# Optimizing a Trainium2 kernel written in Bass

```python
import numpy as np
import jax
import jax.numpy as jnp

def _softmax(x, axis=-1):
    return jax.nn.softmax(x, axis=axis)

def _gelu(x):
    return jax.nn.gelu(x, approximate=True)

def _silu(x):
    return jax.nn.silu(x)

def _sigmoid(x):
    return jax.nn.sigmoid(x)

def _layernorm(x, axis=-1, eps=1e-05):
    m = jnp.mean(x, axis=axis, keepdims=True)
    v = jnp.var(x, axis=axis, keepdims=True)
    return (x - m) / jnp.sqrt(v + eps)

def _scatter_add(tgt, idx, src, axis=0):
    return tgt.at[idx].add(src)

def _segment_sum(src, seg, n):
    return jax.ops.segment_sum(src, seg, n)
kernel_name = 'mk_xattn_seq_d2_seqx_r4_4c130d'

def setup_inputs(seed: int=0):
    np.random.seed(seed)
    _w = jnp.asarray

    def _rec_inputs():
        import jax
        import jax.numpy as jnp
        _rk = jax.random.key(seed)
        x = -0.0002928 + 1 * jax.random.normal(jax.random.fold_in(_rk, 1), (4, 512, 512), jnp.float32)
        _lenS = 512 - jax.random.randint(jax.random.fold_in(_rk, 7), (4,), 0, max(1, 512 // 4) + 1, jnp.int32)
        _lenS2 = 512 - jax.random.randint(jax.random.fold_in(_rk, 8), (4,), 0, max(1, 512 // 4) + 1, jnp.int32)
        _ctx_2048P = jax.random.normal(jax.random.fold_in(_rk, 11), (4, 16, 512), jnp.float32)
        _ctx_2048c = jax.random.dirichlet(jax.random.fold_in(_rk, 511), 0.3 * jnp.ones((16,), jnp.float32), (4, 512))
        _ctx_2048t = jnp.einsum('bsk,bkd->bsd', _ctx_2048c, _ctx_2048P)
        _ctx_2048t = _ctx_2048t * jax.lax.rsqrt(jnp.mean(jnp.square(_ctx_2048t)) + 1e-12) * 0.953939
        ctx_2048 = 0.000189249 + 0.0999589 * (_ctx_2048t + 0.3 * jax.random.normal(jax.random.fold_in(_rk, 611), (4, 512, 512), jnp.float32))
        return (x, ctx_2048)
    x, ctx_2048 = _rec_inputs()

    def _L0_xattn_setup():
        import jax, jax.numpy as jnp
        import numpy as np
        B, L, E, H = (4, 128, 512, 32)
        S = E // H
        EXTRA_MAA, EXTRA_DECAY = (32, 64)
        EPS = 1e-05

        def _ln(x, w, b):
            m = jnp.mean(x, axis=-1, keepdims=True)
            v = jnp.mean((x - m) ** 2, axis=-1, keepdims=True)
            return (x - m) * jax.lax.rsqrt(v + EPS) * w + b

        def _token_shift(xn, prev_row):
            first = (prev_row - xn[:, 0])[:, None]
            rest = xn[:, :-1] - xn[:, 1:]
            return jnp.concatenate([first, rest], axis=1)
        key = jax.random.key(seed)
        ks = jax.random.split(key, 24)
        rn = lambda k, shp, s=1.0: jax.random.normal(k, shp, dtype=jnp.float32) * s
        return dict(x=rn(ks[0], (B, L, E)), state=rn(ks[1], (B, 2 + S, E), 0.1), ln1_w=jnp.ones((E,), jnp.float32), ln1_b=jnp.zeros((E,), jnp.float32), ln2_w=jnp.ones((E,), jnp.float32), ln2_b=jnp.zeros((E,), jnp.float32), maa_x=rn(ks[2], (E,), 0.02), maa_w1=rn(ks[3], (E, 5 * EXTRA_MAA), 0.02), maa_w2=rn(ks[4], (5, EXTRA_MAA, E), 0.02), maa_stack=rn(ks[5], (5, E), 0.02), time_decay=rn(ks[6], (E,), 0.5), decay_w1=rn(ks[7], (E, EXTRA_DECAY), 0.02), decay_w2=rn(ks[8], (EXTRA_DECAY, E), 0.02), faaaa=rn(ks[9], (H, S), 0.1), Wr=rn(ks[10], (E, E), 0.02), Wk=rn(ks[11], (E, E), 0.02), Wv=rn(ks[12], (E, E), 0.02), Wg=rn(ks[13], (E, E), 0.02), Wo=rn(ks[14], (E, E), 0.02), gn_w=jnp.ones((E,), jnp.float32), gn_b=jnp.zeros((E,), jnp.float32), ffn_maa_k=rn(ks[15], (E,), 0.02), ffn_maa_r=rn(ks[16], (E,), 0.02), ffn_Wk=rn(ks[17], (E, E), 0.02), ffn_Wr=rn(ks[18], (E, E), 0.02), ffn_Wv=rn(ks[19], (E, E), 0.02), i=0)
    _L0_xattn_all = _L0_xattn_setup()
    _L0_xattn_in = {k: v for k, v in _L0_xattn_all.items() if k in ('ln1_w', 'ln1_b', 'ln2_w', 'ln2_b', 'maa_x', 'maa_w1', 'maa_w2', 'maa_stack', 'time_decay', 'decay_w1', 'decay_w2', 'faaaa', 'Wr', 'Wk', 'Wv', 'Wg', 'Wo', 'gn_w', 'gn_b', 'ffn_maa_k', 'ffn_maa_r', 'ffn_Wk', 'ffn_Wr', 'ffn_Wv')}
    del _L0_xattn_all

    def _L1_xattn_setup():
        import jax, jax.numpy as jnp
        import numpy as np
        N_HEAD = 32
        EPS = 1e-05

        def _ln(x, w, b):
            m = jnp.mean(x, axis=-1, keepdims=True)
            v = jnp.mean((x - m) ** 2, axis=-1, keepdims=True)
            return (x - m) * jax.lax.rsqrt(v + EPS) * w + b

        def _forward(x, state, i, ln1_w, ln1_b, ln2_w, ln2_b, maa_x, maa_w, maa_k, maa_v, maa_r, maa_g, maa_w1, maa_w2, time_decay, decay_w1, decay_w2, faaaa, Wr, Wk, Wv, Wg, Wo, gn_w, gn_b, fmaa_k, fmaa_r, fWk, fWr, fWv):
            B, L, C = x.shape
            H = N_HEAD
            S = C // H
            i0 = (2 + S) * i
            xa = _ln(x, ln1_w, ln1_b)
            sx = jnp.concatenate([state[:, i0 + 1][:, None], xa[:, :-1]], axis=1) - xa
            xxx = xa + sx * maa_x
            t = jnp.tanh(xxx @ maa_w1).reshape(B, L, 5, -1)
            m = jnp.einsum('blfd,fdc->blfc', t, maa_w2)
            mw, mk, mv, mr, mg = (m[:, :, j] for j in range(5))
            xw = xa + sx * (maa_w + mw)
            xk = xa + sx * (maa_k + mk)
            xv = xa + sx * (maa_v + mv)
            xr = xa + sx * (maa_r + mr)
            xg = xa + sx * (maa_g + mg)
            w = time_decay + jnp.tanh(xw @ decay_w1) @ decay_w2
            w = jnp.exp(-jnp.exp(w)).reshape(B, L, H, S)
            r = (xr @ Wr.T).reshape(B, L, H, S)
            k = (xk @ Wk.T).reshape(B, L, H, S)
            v = (xv @ Wv.T).reshape(B, L, H, S)
            g = jax.nn.silu(xg @ Wg.T)
            s0 = state[:, i0 + 2:i0 + 2 + S].reshape(B, H, S, S)

            def step(s, inp):
                k_l, v_l, w_l, r_l = inp
                a = k_l[..., :, None] * v_l[..., None, :]
                out = jnp.einsum('bhs,bhst->bht', r_l, faaaa * a + s)
                s_new = a + w_l[..., None] * s
                return (s_new, out)
            seq = tuple((z.transpose(1, 0, 2, 3) for z in (k, v, w, r)))
            _, outs = jax.lax.scan(step, s0, seq)
            y = outs.transpose(1, 0, 2, 3)
            gm = jnp.mean(y, axis=-1, keepdims=True)
            gv = jnp.mean((y - gm) ** 2, axis=-1, keepdims=True)
            y = ((y - gm) * jax.lax.rsqrt(gv + EPS)).reshape(B, L, C) * gn_w + gn_b
            x = x + y * g @ Wo.T
            xc = _ln(x, ln2_w, ln2_b)
            sxc = jnp.concatenate([state[:, i0][:, None], xc[:, :-1]], axis=1) - xc
            xk2 = xc + sxc * fmaa_k
            xr2 = xc + sxc * fmaa_r
            rr = jax.nn.sigmoid(xr2 @ fWr.T)
            kk = jnp.square(jax.nn.relu(xk2 @ fWk.T))
            x = x + rr * (kk @ fWv.T)
            return x
        key = jax.random.key(seed)
        B, L, C, H = (8, 128, 512, N_HEAD)
        S = C // H
        DM, DD = (32, 64)
        ks = jax.random.split(key, 32)
        n = lambda k, shp, s=1.0: jax.random.normal(k, shp, dtype=jnp.float32) * s
        u = lambda k, shp: jax.random.uniform(k, shp, dtype=jnp.float32)
        inp = {'x': n(ks[0], (B, L, C)), 'state': n(ks[1], (B, 2 + S, C), 0.1), 'i': 0, 'ln1_w': jnp.ones((C,), jnp.float32), 'ln1_b': jnp.zeros((C,), jnp.float32), 'ln2_w': jnp.ones((C,), jnp.float32), 'ln2_b': jnp.zeros((C,), jnp.float32), 'maa_x': u(ks[2], (C,)), 'maa_w': u(ks[3], (C,)), 'maa_k': u(ks[4], (C,)), 'maa_v': u(ks[5], (C,)), 'maa_r': u(ks[6], (C,)), 'maa_g': u(ks[7], (C,)), 'maa_w1': n(ks[8], (C, 5 * DM), 0.02), 'maa_w2': n(ks[9], (5, DM, C), 0.02), 'time_decay': n(ks[10], (C,), 0.5), 'decay_w1': n(ks[11], (C, DD), 0.02), 'decay_w2': n(ks[12], (DD, C), 0.02), 'faaaa': n(ks[13], (H, S, 1), 0.1), 'Wr': n(ks[14], (C, C), 0.02), 'Wk': n(ks[15], (C, C), 0.02), 'Wv': n(ks[16], (C, C), 0.02), 'Wg': n(ks[17], (C, C), 0.02), 'Wo': n(ks[18], (C, C), 0.02), 'gn_w': jnp.ones((C,), jnp.float32), 'gn_b': jnp.zeros((C,), jnp.float32), 'fmaa_k': u(ks[19], (C,)), 'fmaa_r': u(ks[20], (C,)), 'fWk': n(ks[21], (C, C), 0.02), 'fWr': n(ks[22], (C, C), 0.02), 'fWv': n(ks[23], (C, C), 0.02)}
        return inp
    _L1_xattn_all = _L1_xattn_setup()
    _L1_xattn_in = {k: v for k, v in _L1_xattn_all.items() if k in ('ln1_w', 'ln1_b', 'ln2_w', 'ln2_b', 'maa_x', 'maa_w', 'maa_k', 'maa_v', 'maa_r', 'maa_g', 'maa_w1', 'maa_w2', 'time_decay', 'decay_w1', 'decay_w2', 'faaaa', 'Wr', 'Wk', 'Wv', 'Wg', 'Wo', 'gn_w', 'gn_b', 'fmaa_k', 'fmaa_r', 'fWk', 'fWr', 'fWv')}
    del _L1_xattn_all
    return {'x': x, 'ctx_2048': ctx_2048, 'L0_xattn_ln1_w': _L0_xattn_in['ln1_w'], 'L0_xattn_ln1_b': _L0_xattn_in['ln1_b'], 'L0_xattn_ln2_w': _L0_xattn_in['ln2_w'], 'L0_xattn_ln2_b': _L0_xattn_in['ln2_b'], 'L0_xattn_maa_x': _L0_xattn_in['maa_x'], 'L0_xattn_maa_w1': _L0_xattn_in['maa_w1'], 'L0_xattn_maa_w2': _L0_xattn_in['maa_w2'], 'L0_xattn_maa_stack': _L0_xattn_in['maa_stack'], 'L0_xattn_time_decay': _L0_xattn_in['time_decay'], 'L0_xattn_decay_w1': _L0_xattn_in['decay_w1'], 'L0_xattn_decay_w2': _L0_xattn_in['decay_w2'], 'L0_xattn_faaaa': _L0_xattn_in['faaaa'], 'L0_xattn_Wr': _L0_xattn_in['Wr'], 'L0_xattn_Wk': _L0_xattn_in['Wk'], 'L0_xattn_Wv': _L0_xattn_in['Wv'], 'L0_xattn_Wg': _L0_xattn_in['Wg'], 'L0_xattn_Wo': _L0_xattn_in['Wo'], 'L0_xattn_gn_w': _L0_xattn_in['gn_w'], 'L0_xattn_gn_b': _L0_xattn_in['gn_b'], 'L0_xattn_ffn_maa_k': _L0_xattn_in['ffn_maa_k'], 'L0_xattn_ffn_maa_r': _L0_xattn_in['ffn_maa_r'], 'L0_xattn_ffn_Wk': _L0_xattn_in['ffn_Wk'], 'L0_xattn_ffn_Wr': _L0_xattn_in['ffn_Wr'], 'L0_xattn_ffn_Wv': _L0_xattn_in['ffn_Wv'], 'L1_xattn_ln1_w': _L1_xattn_in['ln1_w'], 'L1_xattn_ln1_b': _L1_xattn_in['ln1_b'], 'L1_xattn_ln2_w': _L1_xattn_in['ln2_w'], 'L1_xattn_ln2_b': _L1_xattn_in['ln2_b'], 'L1_xattn_maa_x': _L1_xattn_in['maa_x'], 'L1_xattn_maa_w': _L1_xattn_in['maa_w'], 'L1_xattn_maa_k': _L1_xattn_in['maa_k'], 'L1_xattn_maa_v': _L1_xattn_in['maa_v'], 'L1_xattn_maa_r': _L1_xattn_in['maa_r'], 'L1_xattn_maa_g': _L1_xattn_in['maa_g'], 'L1_xattn_maa_w1': _L1_xattn_in['maa_w1'], 'L1_xattn_maa_w2': _L1_xattn_in['maa_w2'], 'L1_xattn_time_decay': _L1_xattn_in['time_decay'], 'L1_xattn_decay_w1': _L1_xattn_in['decay_w1'], 'L1_xattn_decay_w2': _L1_xattn_in['decay_w2'], 'L1_xattn_faaaa': _L1_xattn_in['faaaa'], 'L1_xattn_Wr': _L1_xattn_in['Wr'], 'L1_xattn_Wk': _L1_xattn_in['Wk'], 'L1_xattn_Wv': _L1_xattn_in['Wv'], 'L1_xattn_Wg': _L1_xattn_in['Wg'], 'L1_xattn_Wo': _L1_xattn_in['Wo'], 'L1_xattn_gn_w': _L1_xattn_in['gn_w'], 'L1_xattn_gn_b': _L1_xattn_in['gn_b'], 'L1_xattn_fmaa_k': _L1_xattn_in['fmaa_k'], 'L1_xattn_fmaa_r': _L1_xattn_in['fmaa_r'], 'L1_xattn_fWk': _L1_xattn_in['fWk'], 'L1_xattn_fWr': _L1_xattn_in['fWr'], 'L1_xattn_fWv': _L1_xattn_in['fWv']}

def reference(x, ctx_2048, L0_xattn_ln1_w, L0_xattn_ln1_b, L0_xattn_ln2_w, L0_xattn_ln2_b, L0_xattn_maa_x, L0_xattn_maa_w1, L0_xattn_maa_w2, L0_xattn_maa_stack, L0_xattn_time_decay, L0_xattn_decay_w1, L0_xattn_decay_w2, L0_xattn_faaaa, L0_xattn_Wr, L0_xattn_Wk, L0_xattn_Wv, L0_xattn_Wg, L0_xattn_Wo, L0_xattn_gn_w, L0_xattn_gn_b, L0_xattn_ffn_maa_k, L0_xattn_ffn_maa_r, L0_xattn_ffn_Wk, L0_xattn_ffn_Wr, L0_xattn_ffn_Wv, L1_xattn_ln1_w, L1_xattn_ln1_b, L1_xattn_ln2_w, L1_xattn_ln2_b, L1_xattn_maa_x, L1_xattn_maa_w, L1_xattn_maa_k, L1_xattn_maa_v, L1_xattn_maa_r, L1_xattn_maa_g, L1_xattn_maa_w1, L1_xattn_maa_w2, L1_xattn_time_decay, L1_xattn_decay_w1, L1_xattn_decay_w2, L1_xattn_faaaa, L1_xattn_Wr, L1_xattn_Wk, L1_xattn_Wv, L1_xattn_Wg, L1_xattn_Wo, L1_xattn_gn_w, L1_xattn_gn_b, L1_xattn_fmaa_k, L1_xattn_fmaa_r, L1_xattn_fWk, L1_xattn_fWr, L1_xattn_fWv):
    import jax
    import jax.numpy as jnp

    def _L0_xattn_ref(x, state, ln1_w, ln1_b, ln2_w, ln2_b, maa_x, maa_w1, maa_w2, maa_stack, time_decay, decay_w1, decay_w2, faaaa, Wr, Wk, Wv, Wg, Wo, gn_w, gn_b, ffn_maa_k, ffn_maa_r, ffn_Wk, ffn_Wr, ffn_Wv, i):
        import jax, jax.numpy as jnp
        import numpy as np
        B, L, E, H = (4, 128, 512, 32)
        S = E // H
        EXTRA_MAA, EXTRA_DECAY = (32, 64)
        EPS = 1e-05

        def _ln(x, w, b):
            m = jnp.mean(x, axis=-1, keepdims=True)
            v = jnp.mean((x - m) ** 2, axis=-1, keepdims=True)
            return (x - m) * jax.lax.rsqrt(v + EPS) * w + b

        def _token_shift(xn, prev_row):
            first = (prev_row - xn[:, 0])[:, None]
            rest = xn[:, :-1] - xn[:, 1:]
            return jnp.concatenate([first, rest], axis=1)
        b, l = (x.shape[0], x.shape[1])
        i0 = (2 + S) * i + 0
        i1 = (2 + S) * i + 1
        xn = _ln(x, ln1_w, ln1_b)
        sx = _token_shift(xn, state[:, i1])
        xxx = jnp.tanh((xn + sx * maa_x) @ maa_w1).reshape(b, l, 5, 1, EXTRA_MAA)
        xxx = jnp.matmul(xxx, maa_w2).reshape(b, l, 5, E)
        x5 = xn[:, :, None] + sx[:, :, None] * (maa_stack + xxx)
        w = jnp.exp(-jnp.exp(time_decay + jnp.tanh(x5[:, :, 1] @ decay_w1) @ decay_w2))
        w = w.reshape(b, l, H, S)
        r = (x5[:, :, 3] @ Wr.T).reshape(b, l, H, S)
        k = (x5[:, :, 0] @ Wk.T).reshape(b, l, H, S)
        v = (x5[:, :, 2] @ Wv.T).reshape(b, l, H, S)
        g = jax.nn.silu(x5[:, :, 4] @ Wg.T)
        s0 = state[:, (2 + S) * i + 2:(2 + S) * (i + 1)].reshape(b, H, S, S)
        u = faaaa[None, :, :, None]

        def step(s, rkvw):
            r_t, k_t, v_t, w_t = rkvw
            a = k_t[:, :, :, None] * v_t[:, :, None, :]
            out = jnp.einsum('bhk,bhkd->bhd', r_t, u * a + s)
            return (a + w_t[:, :, :, None] * s, out)
        xs = tuple((jnp.moveaxis(t, 1, 0) for t in (r, k, v, w)))
        _, outs = jax.lax.scan(step, s0, xs)
        att = jnp.moveaxis(outs, 0, 1).reshape(b, l, E)
        a4 = att.reshape(b, l, H, S)
        m = jnp.mean(a4, axis=-1, keepdims=True)
        var = jnp.mean((a4 - m) ** 2, axis=-1, keepdims=True)
        att = ((a4 - m) * jax.lax.rsqrt(var + EPS)).reshape(b, l, E) * gn_w + gn_b
        x = x + att * g @ Wo.T
        xn2 = _ln(x, ln2_w, ln2_b)
        sx2 = _token_shift(xn2, state[:, i0])
        xk = xn2 + sx2 * ffn_maa_k
        xr = xn2 + sx2 * ffn_maa_r
        rr = jax.nn.sigmoid(xr @ ffn_Wr.T)
        kk = jnp.square(jax.nn.relu(xk @ ffn_Wk.T))
        x = x + rr * (kk @ ffn_Wv.T)
        return x

    def _L1_xattn_ref(x, state, i, ln1_w, ln1_b, ln2_w, ln2_b, maa_x, maa_w, maa_k, maa_v, maa_r, maa_g, maa_w1, maa_w2, time_decay, decay_w1, decay_w2, faaaa, Wr, Wk, Wv, Wg, Wo, gn_w, gn_b, fmaa_k, fmaa_r, fWk, fWr, fWv):
        import jax, jax.numpy as jnp
        import numpy as np
        N_HEAD = 32
        EPS = 1e-05

        def _ln(x, w, b):
            m = jnp.mean(x, axis=-1, keepdims=True)
            v = jnp.mean((x - m) ** 2, axis=-1, keepdims=True)
            return (x - m) * jax.lax.rsqrt(v + EPS) * w + b

        def _forward(x, state, i, ln1_w, ln1_b, ln2_w, ln2_b, maa_x, maa_w, maa_k, maa_v, maa_r, maa_g, maa_w1, maa_w2, time_decay, decay_w1, decay_w2, faaaa, Wr, Wk, Wv, Wg, Wo, gn_w, gn_b, fmaa_k, fmaa_r, fWk, fWr, fWv):
            B, L, C = x.shape
            H = N_HEAD
            S = C // H
            i0 = (2 + S) * i
            xa = _ln(x, ln1_w, ln1_b)
            sx = jnp.concatenate([state[:, i0 + 1][:, None], xa[:, :-1]], axis=1) - xa
            xxx = xa + sx * maa_x
            t = jnp.tanh(xxx @ maa_w1).reshape(B, L, 5, -1)
            m = jnp.einsum('blfd,fdc->blfc', t, maa_w2)
            mw, mk, mv, mr, mg = (m[:, :, j] for j in range(5))
            xw = xa + sx * (maa_w + mw)
            xk = xa + sx * (maa_k + mk)
            xv = xa + sx * (maa_v + mv)
            xr = xa + sx * (maa_r + mr)
            xg = xa + sx * (maa_g + mg)
            w = time_decay + jnp.tanh(xw @ decay_w1) @ decay_w2
            w = jnp.exp(-jnp.exp(w)).reshape(B, L, H, S)
            r = (xr @ Wr.T).reshape(B, L, H, S)
            k = (xk @ Wk.T).reshape(B, L, H, S)
            v = (xv @ Wv.T).reshape(B, L, H, S)
            g = jax.nn.silu(xg @ Wg.T)
            s0 = state[:, i0 + 2:i0 + 2 + S].reshape(B, H, S, S)

            def step(s, inp):
                k_l, v_l, w_l, r_l = inp
                a = k_l[..., :, None] * v_l[..., None, :]
                out = jnp.einsum('bhs,bhst->bht', r_l, faaaa * a + s)
                s_new = a + w_l[..., None] * s
                return (s_new, out)
            seq = tuple((z.transpose(1, 0, 2, 3) for z in (k, v, w, r)))
            _, outs = jax.lax.scan(step, s0, seq)
            y = outs.transpose(1, 0, 2, 3)
            gm = jnp.mean(y, axis=-1, keepdims=True)
            gv = jnp.mean((y - gm) ** 2, axis=-1, keepdims=True)
            y = ((y - gm) * jax.lax.rsqrt(gv + EPS)).reshape(B, L, C) * gn_w + gn_b
            x = x + y * g @ Wo.T
            xc = _ln(x, ln2_w, ln2_b)
            sxc = jnp.concatenate([state[:, i0][:, None], xc[:, :-1]], axis=1) - xc
            xk2 = xc + sxc * fmaa_k
            xr2 = xc + sxc * fmaa_r
            rr = jax.nn.sigmoid(xr2 @ fWr.T)
            kk = jnp.square(jax.nn.relu(xk2 @ fWk.T))
            x = x + rr * (kk @ fWv.T)
            return x
        return _forward(x, state, i, ln1_w, ln1_b, ln2_w, ln2_b, maa_x, maa_w, maa_k, maa_v, maa_r, maa_g, maa_w1, maa_w2, time_decay, decay_w1, decay_w2, faaaa, Wr, Wk, Wv, Wg, Wo, gn_w, gn_b, fmaa_k, fmaa_r, fWk, fWr, fWv)
    x = _L0_xattn_ref(x, ctx_2048, L0_xattn_ln1_w, L0_xattn_ln1_b, L0_xattn_ln2_w, L0_xattn_ln2_b, L0_xattn_maa_x, L0_xattn_maa_w1, L0_xattn_maa_w2, L0_xattn_maa_stack, L0_xattn_time_decay, L0_xattn_decay_w1, L0_xattn_decay_w2, L0_xattn_faaaa, L0_xattn_Wr, L0_xattn_Wk, L0_xattn_Wv, L0_xattn_Wg, L0_xattn_Wo, L0_xattn_gn_w, L0_xattn_gn_b, L0_xattn_ffn_maa_k, L0_xattn_ffn_maa_r, L0_xattn_ffn_Wk, L0_xattn_ffn_Wr, L0_xattn_ffn_Wv, 0)
    x = _L1_xattn_ref(x, ctx_2048, 0, L1_xattn_ln1_w, L1_xattn_ln1_b, L1_xattn_ln2_w, L1_xattn_ln2_b, L1_xattn_maa_x, L1_xattn_maa_w, L1_xattn_maa_k, L1_xattn_maa_v, L1_xattn_maa_r, L1_xattn_maa_g, L1_xattn_maa_w1, L1_xattn_maa_w2, L1_xattn_time_decay, L1_xattn_decay_w1, L1_xattn_decay_w2, L1_xattn_faaaa, L1_xattn_Wr, L1_xattn_Wk, L1_xattn_Wv, L1_xattn_Wg, L1_xattn_Wo, L1_xattn_gn_w, L1_xattn_gn_b, L1_xattn_fmaa_k, L1_xattn_fmaa_r, L1_xattn_fWk, L1_xattn_fWr, L1_xattn_fWv)
    return x

_drawn_inputs = setup_inputs


def setup_inputs(seed=0):
    import zlib

    import numpy as np

    out = dict(_drawn_inputs(seed))
    spreads = {'L0_xattn_ln1_w': (1.0, 0.2),
     'L0_xattn_ln1_b': (0.0, 0.1),
     'L0_xattn_ln2_w': (1.0, 0.6),
     'L0_xattn_ln2_b': (0.0, 0.8),
     'L0_xattn_gn_w': (1.0, 0.6),
     'L0_xattn_gn_b': (0.0, 0.656),
     'L1_xattn_ln1_w': (1.0, 0.2),
     'L1_xattn_ln1_b': (0.0, 0.286),
     'L1_xattn_ln2_w': (1.0, 0.6),
     'L1_xattn_ln2_b': (0.0, 0.8),
     'L1_xattn_gn_w': (1.0, 0.6),
     'L1_xattn_gn_b': (0.0, 0.8)}
    factors = {'ctx_2048': 27.09,
     'L0_xattn_maa_x': 8.0,
     'L0_xattn_maa_w1': 2.798,
     'L0_xattn_maa_w2': 2.819,
     'L0_xattn_maa_stack': 6.138,
     'L0_xattn_decay_w1': 8.0,
     'L0_xattn_decay_w2': 8.0,
     'L0_xattn_faaaa': 2.901,
     'L0_xattn_ffn_maa_k': 8.0,
     'L0_xattn_ffn_maa_r': 8.0,
     'L0_xattn_ffn_Wr': 4.016,
     'L1_xattn_maa_x': 6.762,
     'L1_xattn_maa_w': 8.0,
     'L1_xattn_maa_w1': 3.486,
     'L1_xattn_maa_w2': 3.535,
     'L1_xattn_decay_w1': 8.0,
     'L1_xattn_decay_w2': 8.0,
     'L1_xattn_faaaa': 3.759,
     'L1_xattn_fmaa_r': 8.0,
     'L1_xattn_fWr': 7.647}
    for name, (base, spread) in spreads.items():
        noise = np.random.default_rng([zlib.crc32(name.encode()), seed]).standard_normal(out[name].shape)
        drawn = base * np.exp(spread * noise) if base else spread * noise
        out[name] = jnp.asarray(drawn.astype(out[name].dtype))
    for name, factor in factors.items():
        out[name] = (out[name] * factor).astype(out[name].dtype)
    return out
```

```python
import numpy as np
import concourse.bass as bass
from concourse import mybir
from contextlib import ExitStack

F32 = mybir.dt.float32
ALU = mybir.AluOpType
ACT = mybir.ActivationFunctionType

P = 128
LAYERS, B, T, C = 2, 4, 512, 512
H, S = 32, 16
CT, TT = C // P, T // P
DM, DD, NF = 32, 64, 5
EPS = 1e-5
VG = 4
GROUPS = S // VG
SLOTS = 3
NGROUP = CT * GROUPS

BW, BK, BR, BV, BG = range(NF)
LN1W, LN1B, MAAX, MAAW, MAAK, MAAR, MAAV, MAAG, TDECAY, UBONUS = range(10)
NVA = 10
MAA = {BW: MAAW, BK: MAAK, BR: MAAR, BV: MAAV, BG: MAAG}
GNW, GNB, LN2W, LN2B, FMK, FMR = range(6)
NVF = 6
WK, WR, WV, WG = range(4)
WO, FK, FR, FV = range(4)
IDENT, HMEAN, CENTRE, HONES, REDUCE = 0, 1, 2, 3, 4
NCONST = REDUCE + S

WORK = 4
JOBS = []
JOBS += [("xa", c) for c in range(CT)]
JOBS += [("maa_hidden", 0), ("maa_hidden", 1)]
JOBS += [("mix", BW, c) for c in range(CT)] + [("mix", BK, c) for c in range(CT)]
JOBS += [("decay_hidden",)]
JOBS += [("mix", f, c) for f in (BR, BV, BG) for c in range(CT)]
for _c in range(CT + 1):
    if _c < CT:
        JOBS += [("w", _c), ("k", _c), ("r", _c), ("v", _c)]
    if _c > 0:
        JOBS += [("g", _c - 1)]
JOBS += [("wo", t) for t in range(TT)]
JOBS += [("xc", c) for c in range(CT)]
JOBS += [("fk", c) for c in range(CT)]
JOBS += [("fr", t) for t in range(TT)]
JOBS += [("fv", t) for t in range(TT)]
BANK = {job: i % WORK for i, job in enumerate(JOBS)}
TURN = {job: i // WORK for i, job in enumerate(JOBS)}
PER_BANK = [sum(BANK[j] == b for j in JOBS) for b in range(WORK)]
MIX_ORDER = [(f, c) for f in (BW, BK, BR, BV, BG) for c in range(CT)]


class Flag:

    def __init__(self, sem, per, primed=0):
        self.sem, self.per, self.primed = sem, per, primed

    def wait(self, engine, it, n):
        engine.wait_ge(self.sem, it * self.per + (n + self.primed))


def build(nc, x, weights_a, weights_f, maa_w1, maa_w2, decay_w1, decay_w2, vectors_a, vectors_f, prev, s0, consts, out):
    ctx = ExitStack()
    with ctx:
        def sb(name, shape):
            return ctx.enter_context(nc.sbuf_tensor(name, shape, F32))

        def flag(name, per=1, primed=0):
            return Flag(ctx.enter_context(nc.semaphore(name)), per, primed)

        wa = sb("wa", [P, 4, CT, C])
        wf = sb("wf", [P, 4, CT, C])
        mw1 = sb("mw1", [P, CT, NF * DM])
        mw2 = sb("mw2", [P, 2, C])
        dw1 = sb("dw1", [P, CT, DD])
        dw2 = sb("dw2", [DD, C])
        va = sb("va", [P, NVA, CT])
        vf = sb("vf", [P, NVF, CT])
        bonus = sb("bonus", [P, CT, P])
        cst = sb("cst", [P, NCONST, P])
        pv = sb("pv", [P, B, 2, CT])
        st0 = sb("st0", [P, B, CT, S])
        xres = sb("xres", [P, TT, C])
        xa = sb("xa", [P, CT, T + 1])
        sx = sb("sx", [P, CT, T])
        mixed = sb("mixed", [P, 4, CT, T])
        hid = sb("hid", [P, T])
        hid4 = sb("hid4", [DM, T])
        dhid = sb("dhid", [DD, T])
        kt = sb("kt", [P, 2, T])
        rt = sb("rt", [P, 2, T])
        vt = sb("vt", [P, 2, T])
        wt = sb("wt", [P, 2, T])
        ring = sb("ring", [P, SLOTS, VG, T])
        states = sb("states", [P, VG, T])
        rk = sb("rk", [P, T])
        uv = sb("uv", [P, T])
        sq = sb("sq", [P, T])
        yn = sb("yn", [P, T])
        stats = sb("stats", [P, TT, 6])
        mv = sb("mv", [P, TT, 2])
        vareps = sb("vareps", [P, TT])
        power = sb("power", [P, TT])
        rstd = sb("rstd", [P, TT])
        eps = sb("eps", [P, 1])
        srow = sb("srow", [P, CT, S])

        xn = ring[:, 1]
        normed = mixed[:, 0]
        xxx = mixed[:, 1]
        SLOT = {BK: 0, BR: 1, BV: 2, BW: 3, BG: 3}
        gate = sx
        yg = xa
        sig = mixed[:, 3]
        xk2, xr2, kk, rr = (mixed[:, i] for i in range(4))
        scratch = [rk, uv]

        work = [ctx.enter_context(nc.psum_tensor(f"work{i}", [P, 512], F32)) for i in range(WORK)]
        py = [ctx.enter_context(nc.psum_tensor(f"py{i}", [P, 512], F32)) for i in range(2)]
        pbonus = ctx.enter_context(nc.psum_tensor("pbonus", [P, 512], F32))
        pvar = ctx.enter_context(nc.psum_tensor("pvar", [P, 512], F32))

        full = [flag(f"work_full{b}", PER_BANK[b]) for b in range(WORK)]
        consts_in = flag("consts_in")
        gates_passed = flag("gates_passed")
        power_ready = flag("power_ready")
        weights_a_in = flag("weights_a_in")
        weights_f_in = flag("weights_f_in")
        batch_done = flag("batch_done", TT, primed=1)
        bonus_ready = flag("bonus_ready")
        home = flag("home", 16)
        xn_in = flag("xn_in", 16)
        xres_in = flag("xres_in", 16)
        stats_done = flag("stats_done", 2 * TT)
        moments_done = flag("moments_done", 2 * TT)
        vareps_ready = flag("vareps_ready", 2)
        rstd_done = flag("rstd_done", 2)
        normed_ready = flag("normed_ready", 2 * TT)
        prev_ready = flag("prev_ready", 2)
        s0_ready = flag("s0_ready")
        xa_ready = flag("xa_ready", CT)
        sx_ready = flag("sx_ready", 2)
        xxx_ready = flag("xxx_ready", CT)
        hid_ready = flag("hid_ready", 2)
        dhid_ready = flag("dhid_ready")
        mterm_done = flag("mterm_done", NF * CT)
        mix_ready = flag("mix_ready", NF * CT)
        exp_done = flag("exp_done", CT)
        w_ready = flag("w_ready", CT)
        k_ready = flag("k_ready", CT)
        r_ready = flag("r_ready", CT)
        v_ready = flag("v_ready", CT)
        rk_ready = flag("rk_ready", CT)
        bonus_sum = flag("bonus_sum", CT)
        uv_ready = flag("uv_ready", CT)
        uses = [len(range(s, NGROUP, SLOTS)) for s in range(SLOTS)]
        vb_in = [flag(f"vb_in{s}", uses[s] * VG * 16) for s in range(SLOTS)]
        kv_done = flag("kv_done", NGROUP * 2)
        scan_done = flag("scan_done", NGROUP * VG)
        rs_ready = flag("rs_ready", NGROUP * 3)
        reduced = flag("reduced", NGROUP)
        sq_ready = flag("sq_ready", CT)
        var_ready = flag("var_ready", CT)
        yln_done = flag("yln_done", CT)
        ystd_done = flag("ystd_done", CT)
        yn_ready = flag("yn_ready", CT)
        affine_done = flag("affine_done", CT)
        gate_ready = flag("gate_ready", CT, primed=1)
        yz_done = flag("yz_done", CT)
        sig_ready = flag("sig_ready")
        yg_ready = flag("yg_ready", CT)
        xatt_ready = flag("xatt_ready", TT)
        xc_ready = flag("xc_ready", CT)
        xk2_ready = flag("xk2_ready", CT)
        xr2_ready = flag("xr2_ready", CT)
        relu_done = flag("relu_done", CT)
        kk_ready = flag("kk_ready", CT)
        rr_ready = flag("rr_ready", TT)
        gated_done = flag("gated_done", TT)

        LEFT = {}
        for c in range(CT):
            LEFT["xa", c] = xa_ready, c + 1
            LEFT["w", c] = exp_done, c + 1
            LEFT["k", c] = k_ready, c + 1
            LEFT["r", c] = r_ready, c + 1
            LEFT["v", c] = v_ready, c + 1
            LEFT["g", c] = gate_ready, c + 1
            LEFT["xc", c] = xc_ready, c + 1
            LEFT["fk", c] = relu_done, c + 1
        for t in range(TT):
            LEFT["wo", t] = xatt_ready, t + 1
            LEFT["fr", t] = rr_ready, t + 1
            LEFT["fv", t] = gated_done, t + 1
        for i in range(2):
            LEFT["maa_hidden", i] = hid_ready, i + 1
        for i, (f, c) in enumerate(MIX_ORDER):
            LEFT["mix", f, c] = mterm_done, i + 1
        LEFT["decay_hidden",] = dhid_ready, 1

        out_t = out.rearrange("b (i p) c -> b p i c", p=P)
        x_t = x.rearrange("b (i p) c -> b p i c", p=P)
        DMAS_A, DMAS_F = 5 + 4, 1 + 4

        def bank(job):
            return work[BANK[job]]

        def pass_gate(engine):
            engine.sem_inc(gates_passed.sem, 1)

        def take(engine, it, job):
            full[BANK[job]].wait(engine, it, TURN[job] + 1)

        def spread(c, v):
            rows = vt[:, c % 2]
            step = rows.ap[0][0]
            return bass.AP(rows.tensor, rows.offset + v * step, [[S * step, P // S], [0, S], [1, T]])

        block = ctx.enter_context(nc.Block())

        @block.sync
        def _(sp):
            for tile, src in ((cst, consts), (pv, prev), (st0, s0)):
                sp.dma_start(tile[:], src).then_inc(consts_in.sem, 16)
            with sp.Fori(0, LAYERS) as layer:
                gate_ready.wait(sp, layer * B, 0)
                pass_gate(sp)
                for tile, src in ((va, vectors_a), (mw1, maa_w1), (mw2, maa_w2), (dw1, decay_w1), (dw2, decay_w2)):
                    sp.dma_start(tile[:], src[bass.ds(layer, 1)][0]).then_inc(weights_a_in.sem, 16)
                for i in range(4):
                    sp.dma_start(wa[:, i], weights_a[bass.ds(layer, 1)][0, :, i]).then_inc(weights_a_in.sem, 16)
                batch_done.wait(sp, layer * B, 0)
                pass_gate(sp)
                sp.dma_start(vf[:], vectors_f[bass.ds(layer, 1)][0]).then_inc(weights_f_in.sem, 16)
                for i in range(4):
                    sp.dma_start(wf[:, i], weights_f[bass.ds(layer, 1)][0, :, i]).then_inc(weights_f_in.sem, 16)
                with sp.Fori(0, B) as b:
                    it = layer * B + b
                    for j in range(NGROUP):
                        c, q = j // GROUPS, j % GROUPS
                        if q == 0:
                            v_ready.wait(sp, it, c + 1)
                            pass_gate(sp)
                        if j >= SLOTS:
                            reduced.wait(sp, it, j - SLOTS + 1)
                        for i in range(VG):
                            sp.dma_start(ring[:, j % SLOTS, i], spread(c, VG * q + i)).then_inc(vb_in[j % SLOTS].sem, 16)

        @block.scalar
        def _(act):
            nc.scalar.nop().then_inc(gate_ready.sem, 1)
            act.dma_start(xn, x_t[0]).then_inc(xn_in.sem, 16)
            for b in range(B):
                act.dma_start(out[b], x[b]).then_inc(home.sem, 16)
            act.wait_ge(consts_in.sem, 3 * 16)
            act.wait_ge(power_ready.sem, 2)

            def leave(it, job, dst, func, done, **kw):
                take(act, it, job)
                nc.scalar.activation(dst, bank(job)[0:dst.shape[0], :], func, **kw).then_inc(done.sem, 1)

            def leave_w(it, c):
                leave(it, ("w", c), wt[:, c % 2], ACT.Exp, exp_done, bias=va[:, TDECAY, c:c + 1])
                exp_done.wait(act, it, c + 1)
                nc.scalar.activation(wt[:, c % 2], wt[:, c % 2], ACT.Exp, scale=-1.0).then_inc(w_ready.sem, 1)

            def leave_tile(it, name, c, dst, done):
                leave(it, (name, c), dst[:, c % 2], ACT.Identity, done)

            def square(it, c):
                reduced.wait(act, it, GROUPS * (c + 1))
                if c > 0:
                    var_ready.wait(act, it, c)
                nc.scalar.activation(sq[:], py[c % 2][:], ACT.Square).then_inc(sq_ready.sem, 1)

            def deviation(it, c):
                var_ready.wait(act, it, c + 1)
                if c > 0:
                    yz_done.wait(act, it, c)
                nc.scalar.activation(yn[:], pvar[:], ACT.Ln, bias=eps[:, 0:1]).then_inc(yln_done.sem, 1)
                yln_done.wait(act, it, c + 1)
                nc.scalar.activation(yn[:], yn[:], ACT.Exp, scale=-0.5).then_inc(ystd_done.sem, 1)

            def affine(it, c):
                yn_ready.wait(act, it, c + 1)
                nc.scalar.activation(yn[:], yn[:], ACT.Identity, scale=vf[:, GNW, c:c + 1],
                                     bias=vf[:, GNB, c:c + 1]).then_inc(affine_done.sem, 1)

            with act.Fori(0, LAYERS) as layer:
                act.wait_ge(weights_a_in.sem, layer * (16 * DMAS_A) + 16 * DMAS_A)
                act.wait_ge(weights_f_in.sem, layer * (16 * DMAS_F) + 16 * DMAS_F)
                with act.Fori(0, B) as b:
                    it = layer * B + b
                    nc.scalar.copy(srow[:], st0[:, bass.ds(b, 1)][:, 0]).then_inc(s0_ready.sem, 1)
                    nc.scalar.copy(xa[:, :, 0], pv[:, bass.ds(b, 1)][:, 0, 1]).then_inc(prev_ready.sem, 1)
                    for c in range(CT):
                        leave(it, ("xa", c), xa[:, c, 1:], ACT.Identity, xa_ready,
                              scale=va[:, LN1W, c:c + 1], bias=va[:, LN1B, c:c + 1])
                    leave(it, ("maa_hidden", 0), hid[:], ACT.Tanh, hid_ready)
                    leave(it, ("maa_hidden", 1), hid4[:], ACT.Tanh, hid_ready)
                    leave(it, ("decay_hidden",), dhid[:], ACT.Tanh, dhid_ready)
                    home.wait(act, it, 16 * B)
                    act.dma_start(xres[:], out_t[bass.ds(b, 1)][0]).then_inc(xres_in.sem, 16)
                    leave_w(it, 0)
                    leave_tile(it, "k", 0, kt, k_ready)
                    leave_tile(it, "r", 0, rt, r_ready)
                    leave_tile(it, "v", 0, vt, v_ready)
                    for c in range(CT):
                        if c > 0:
                            square(it, c - 1)
                        if c < CT - 1:
                            if c > 0:
                                rs_ready.wait(act, it, 3 * GROUPS * c)
                            leave_w(it, c + 1)
                            leave_tile(it, "k", c + 1, kt, k_ready)
                        else:
                            leave(it, ("g", c), gate[:, c], ACT.Identity, gate_ready)
                        if c > 0:
                            deviation(it, c - 1)
                        if c < CT - 1:
                            leave_tile(it, "r", c + 1, rt, r_ready)
                        if c > 0:
                            affine(it, c - 1)
                        if c < CT - 1:
                            leave_tile(it, "v", c + 1, vt, v_ready)
                            leave(it, ("g", c), gate[:, c], ACT.Identity, gate_ready)
                    gate_ready.wait(act, it, CT)
                    nc.scalar.activation(sig, gate[:], ACT.Sigmoid).then_inc(sig_ready.sem, 1)
                    square(it, CT - 1)
                    act.dma_start(xn, out_t[bass.ds((b + 1) % B, 1)][0]).then_inc(xn_in.sem, 16)
                    deviation(it, CT - 1)
                    affine(it, CT - 1)
                    take(act, it, ("xc", 0))
                    nc.scalar.copy(xa[:, :, 0], pv[:, bass.ds(b, 1)][:, 0, 0]).then_inc(prev_ready.sem, 1)
                    for c in range(CT):
                        leave(it, ("xc", c), xa[:, c, 1:], ACT.Identity, xc_ready,
                              scale=vf[:, LN2W, c:c + 1], bias=vf[:, LN2B, c:c + 1])
                    for c in range(CT):
                        leave(it, ("fk", c), kk[:, c], ACT.Relu, relu_done)
                        relu_done.wait(act, it, c + 1)
                        nc.scalar.activation(kk[:, c], kk[:, c], ACT.Square).then_inc(kk_ready.sem, 1)
                    for t in range(TT):
                        leave(it, ("fr", t), rr[:, t], ACT.Sigmoid, rr_ready)
                    batch_done.wait(act, it, TT)
                    act.dma_start(out_t[bass.ds(b, 1)][0], xres[:]).then_inc(home.sem, 16)
            act.wait_ge(home.sem, 16 * (B + LAYERS * B))
            act.wait_ge(xn_in.sem, 16 * (1 + LAYERS * B))

        @block.gpsimd
        def _(pool):
            nc.gpsimd.memset(power[:], -0.5).then_inc(power_ready.sem, 1)
            nc.gpsimd.memset(eps[:], EPS).then_inc(power_ready.sem, 1)
            pool.wait_ge(power_ready.sem, 2)
            with pool.Fori(0, 2 * LAYERS * B) as i:
                pool.wait_ge(vareps_ready.sem, i + 1)
                nc.gpsimd.tensor_tensor(rstd[:], vareps[:], power[:], ALU.pow).then_inc(rstd_done.sem, 1)

        @block.vector
        def _(dve):
            nc.vector.nop().then_inc(batch_done.sem, 1)
            dve.wait_ge(consts_in.sem, 3 * 16)

            def normalise(it, half, src):
                n = half * TT
                for t in range(TT):
                    if half:
                        xatt_ready.wait(dve, it, t + 1)
                    nc.vector.bn_stats(stats[:, t], src[:, t]).then_inc(stats_done.sem, 1)
                stats_done.wait(dve, it, n + TT)
                pass_gate(dve)
                for t in range(TT):
                    nc.vector.bn_aggr(mv[:, t], stats[:, t]).then_inc(moments_done.sem, 1)
                moments_done.wait(dve, it, n + TT)
                nc.vector.tensor_scalar(vareps[:], mv[:, :, 1], EPS, None, ALU.add).then_inc(vareps_ready.sem, 1)
                rstd_done.wait(dve, it, half + 1)
                for t in range(TT):
                    nc.vector.tensor_scalar(normed[:, t], src[:, t], mv[:, t, 0:1], rstd[:, t:t + 1],
                                            ALU.subtract, ALU.mult).then_inc(normed_ready.sem, 1)

            def mix_add(it, i):
                f, c = MIX_ORDER[i]
                mterm_done.wait(dve, it, i + 1)
                nc.vector.tensor_tensor(mixed[:, SLOT[f], c], scratch[i % 2][:], xa[:, c, 1:],
                                        ALU.add).then_inc(mix_ready.sem, 1)

            def ynorm(it, c):
                ystd_done.wait(dve, it, c + 1)
                nc.vector.tensor_tensor(yn[:], py[c % 2][:], yn[:], ALU.mult).then_inc(yn_ready.sem, 1)

            def ygate(it, c):
                affine_done.wait(dve, it, c + 1)
                gate_ready.wait(dve, it, c + 1)
                nc.vector.tensor_tensor(yg[:, c, 1:], yn[:], gate[:, c], ALU.mult).then_inc(yz_done.sem, 1)

            def group(it, j):
                c, q = j // GROUPS, j % GROUPS
                s, h = j % SLOTS, c % 2
                vb_in[s].wait(dve, it, (j // SLOTS + 1) * VG * 16)
                for i in range(2):
                    part = ring[:, s, 2 * i:2 * i + 2]
                    nc.vector.tensor_tensor(part, part, kt[:, h:h + 1].broadcast_to([P, 2, T]),
                                            ALU.mult).then_inc(kv_done.sem, 1)
                if q == 0:
                    w_ready.wait(dve, it, c + 1)
                if j > 0:
                    rs_ready.wait(dve, it, 3 * j)
                for i in range(VG):
                    kv_done.wait(dve, it, 2 * j + i // 2 + 1)
                    nc.vector.tensor_tensor_scan(states[:, i], wt[:, h], ring[:, s, i],
                                                 srow[:, c, VG * q + i:VG * q + i + 1],
                                                 ALU.mult, ALU.add).then_inc(scan_done.sem, 1)
                for i in range(2):
                    scan_done.wait(dve, it, VG * j + 2 * i + 2)
                    nc.vector.tensor_tensor(ring[:, s, 2 * i:2 * i + 2, 1:], states[:, 2 * i:2 * i + 2, 0:T - 1],
                                            rt[:, h:h + 1, 1:].broadcast_to([P, 2, T - 1]),
                                            ALU.mult).then_inc(rs_ready.sem, 1)
                nc.vector.tensor_scalar(ring[:, s, :, 0], srow[:, c, VG * q:VG * q + VG], rt[:, h, 0:1], None,
                                        ALU.mult).then_inc(rs_ready.sem, 1)

            with dve.Fori(0, LAYERS) as layer:
                dve.wait_ge(weights_a_in.sem, layer * (16 * DMAS_A) + 16 * DMAS_A)
                dve.wait_ge(weights_f_in.sem, layer * (16 * DMAS_F) + 16 * DMAS_F)
                for c in range(CT):
                    nc.vector.tensor_scalar(bonus[:, c], cst[:, HONES], va[:, UBONUS, c:c + 1], None,
                                            ALU.mult).then_inc(bonus_ready.sem, 1)
                with dve.Fori(0, B) as b:
                    it = layer * B + b
                    xn_in.wait(dve, it, 16)
                    normalise(it, 0, xn)
                    prev_ready.wait(dve, it, 1)
                    xa_ready.wait(dve, it, CT)
                    nc.vector.tensor_tensor(sx[:], xa[:, :, 0:T], xa[:, :, 1:], ALU.subtract).then_inc(sx_ready.sem, 1)
                    sx_ready.wait(dve, it, 1)
                    for c in range(CT):
                        nc.vector.scalar_tensor_tensor(xxx[:, c], sx[:, c], va[:, MAAX, c:c + 1], xa[:, c, 1:],
                                                       ALU.mult, ALU.add).then_inc(xxx_ready.sem, 1)
                    for i, (f, c) in enumerate(MIX_ORDER):
                        take(dve, it, ("mix", f, c))
                        if i >= 2:
                            mix_ready.wait(dve, it, i - 1)
                        if (f, c) == (BG, 0):
                            take(dve, it, ("decay_hidden",))
                        nc.vector.scalar_tensor_tensor(scratch[i % 2][:], bank(("mix", f, c))[:], va[:, MAA[f], c:c + 1],
                                                       sx[:, c], ALU.add, ALU.mult).then_inc(mterm_done.sem, 1)
                        if i > 0:
                            mix_add(it, i - 1)
                    mix_add(it, NF * CT - 1)
                    s0_ready.wait(dve, it, 1)
                    for c in range(CT):
                        k_ready.wait(dve, it, c + 1)
                        r_ready.wait(dve, it, c + 1)
                        v_ready.wait(dve, it, c + 1)
                        if c == 0:
                            mix_ready.wait(dve, it, NF * CT)
                        nc.vector.tensor_tensor(rk[:], rt[:, c % 2], kt[:, c % 2], ALU.mult).then_inc(rk_ready.sem, 1)
                        group(it, GROUPS * c)
                        bonus_sum.wait(dve, it, c + 1)
                        if c > 0:
                            reduced.wait(dve, it, GROUPS * c)
                        nc.vector.tensor_tensor(uv[:], pbonus[:], vt[:, c % 2], ALU.mult).then_inc(uv_ready.sem, 1)
                        group(it, GROUPS * c + 1)
                        if c > 0:
                            ynorm(it, c - 1)
                        group(it, GROUPS * c + 2)
                        if c > 0:
                            ygate(it, c - 1)
                        group(it, GROUPS * c + 3)
                    sig_ready.wait(dve, it, 1)
                    for c in range(CT - 1):
                        yz_done.wait(dve, it, c + 1)
                        nc.vector.tensor_tensor(yg[:, c, 1:], yg[:, c, 1:], sig[:, c], ALU.mult).then_inc(yg_ready.sem, 1)
                    ynorm(it, CT - 1)
                    ygate(it, CT - 1)
                    yz_done.wait(dve, it, CT)
                    nc.vector.tensor_tensor(yg[:, CT - 1, 1:], yg[:, CT - 1, 1:], sig[:, CT - 1],
                                            ALU.mult).then_inc(yg_ready.sem, 1)
                    xres_in.wait(dve, it, 16)
                    for t in range(TT):
                        take(dve, it, ("wo", t))
                        nc.vector.tensor_tensor(xres[:, t], bank(("wo", t))[:], xres[:, t], ALU.add).then_inc(xatt_ready.sem, 1)
                    normalise(it, 1, xres)
                    prev_ready.wait(dve, it, 2)
                    xc_ready.wait(dve, it, CT)
                    nc.vector.tensor_tensor(sx[:], xa[:, :, 0:T], xa[:, :, 1:], ALU.subtract).then_inc(sx_ready.sem, 1)
                    sx_ready.wait(dve, it, 2)
                    for dst, vector, ready in ((xk2, FMK, xk2_ready), (xr2, FMR, xr2_ready)):
                        for c in range(CT):
                            nc.vector.scalar_tensor_tensor(dst[:, c], sx[:, c], vf[:, vector, c:c + 1], xa[:, c, 1:],
                                                           ALU.mult, ALU.add).then_inc(ready.sem, 1)
                    for t in range(TT):
                        take(dve, it, ("fv", t))
                        rr_ready.wait(dve, it, t + 1)
                        if t >= 2:
                            batch_done.wait(dve, it, t - 1)
                        nc.vector.tensor_tensor(scratch[t % 2][:], bank(("fv", t))[:], rr[:, t], ALU.mult).then_inc(gated_done.sem, 1)
                        gated_done.wait(dve, it, t + 1)
                        nc.vector.tensor_tensor(xres[:, t], xres[:, t], scratch[t % 2][:], ALU.add).then_inc(batch_done.sem, 1)

        @block.tensor
        def _(pe):
            pe.wait_ge(consts_in.sem, 3 * 16)

            def enter(it, job):
                if TURN[job] > 0:
                    done, n = LEFT[JOBS[JOBS.index(job) - WORK]]
                    done.wait(pe, it, n)

            def filled(ins, job):
                ins.then_inc(full[BANK[job]].sem, 1)

            def project(it, job, weight, src, column, width=P):
                enter(it, job)
                for i in range(CT):
                    ins = nc.tensor.matmul(bank(job)[0:width, :], weight[:, i, column:column + width], src[:, i],
                                           start=i == 0, stop=i == CT - 1)
                filled(ins, job)

            def project_tokens(it, job, weight, src, t):
                enter(it, job)
                for i in range(CT):
                    ins = nc.tensor.matmul(bank(job)[:], src[:, i, P * t:P * (t + 1)], weight[:, i],
                                           start=i == 0, stop=i == CT - 1)
                filled(ins, job)

            def transposes(it, name, half):
                normed_ready.wait(pe, it, (half + 1) * TT)
                for c in range(CT):
                    enter(it, (name, c))
                    for t in range(TT):
                        ins = nc.tensor.transpose(bank((name, c))[:, P * t:P * (t + 1)], normed[:, t, P * c:P * (c + 1)],
                                                  cst[:, IDENT])
                    filled(ins, (name, c))

            def mixes(it, f):
                for c in range(CT):
                    job = ("mix", f, c)
                    enter(it, job)
                    lo = DM * f if f < 4 else 0
                    src = hid if f < 4 else hid4
                    filled(nc.tensor.matmul(bank(job)[:], mw2[lo:lo + DM, f // 4, P * c:P * (c + 1)], src[lo:lo + DM, :],
                                            start=True, stop=True), job)

            def project_w(it, c):
                dhid_ready.wait(pe, it, 1)
                enter(it, ("w", c))
                filled(nc.tensor.matmul(bank(("w", c))[:], dw2[:, P * c:P * (c + 1)], dhid[:], start=True, stop=True), ("w", c))

            def project_tile(it, name, which, f, c):
                mix_ready.wait(pe, it, (MIX_ORDER.index((f, CT - 1)) + 1))
                project(it, (name, c), wa[:, which], mixed[:, SLOT[f]], P * c)

            def reduce(it, j):
                c, q = j // GROUPS, j % GROUPS
                if q == 0 and c >= 2:
                    yn_ready.wait(pe, it, c - 1)
                rs_ready.wait(pe, it, 3 * (j + 1))
                for i in range(VG):
                    ins = nc.tensor.matmul(py[c % 2][:], cst[:, REDUCE + VG * q + i], ring[:, j % SLOTS, i],
                                           start=q == 0 and i == 0, stop=q == GROUPS - 1 and i == VG - 1)
                ins.then_inc(reduced.sem, 1)

            def variance(it, c):
                sq_ready.wait(pe, it, c + 1)
                if c > 0:
                    yln_done.wait(pe, it, c)
                nc.tensor.matmul(pvar[:], cst[:, HMEAN], sq[:], start=True, stop=True).then_inc(var_ready.sem, 1)

            with pe.Fori(0, LAYERS) as layer:
                pe.wait_ge(weights_a_in.sem, layer * (16 * DMAS_A) + 16 * DMAS_A)
                pe.wait_ge(weights_f_in.sem, layer * (16 * DMAS_F) + 16 * DMAS_F)
                pe.wait_ge(bonus_ready.sem, layer * CT + CT)
                pass_gate(pe)
                with pe.Fori(0, B) as b:
                    it = layer * B + b
                    transposes(it, "xa", 0)
                    xxx_ready.wait(pe, it, CT)
                    project(it, ("maa_hidden", 0), mw1, xxx, 0)
                    project(it, ("maa_hidden", 1), mw1, xxx, P, DM)
                    hid_ready.wait(pe, it, 2)
                    mixes(it, BW)
                    mixes(it, BK)
                    mix_ready.wait(pe, it, CT)
                    project(it, ("decay_hidden",), dw1, mixed[:, SLOT[BW]], 0, DD)
                    for f in (BR, BV, BG):
                        mixes(it, f)
                    project_w(it, 0)
                    project_tile(it, "k", WK, BK, 0)
                    project_tile(it, "r", WR, BR, 0)
                    project_tile(it, "v", WV, BV, 0)
                    for c in range(CT):
                        more = c < CT - 1
                        rk_ready.wait(pe, it, c + 1)
                        if c > 0:
                            uv_ready.wait(pe, it, c)
                        nc.tensor.matmul(pbonus[:], bonus[:, c], rk[:], start=True, stop=True).then_inc(bonus_sum.sem, 1)
                        reduce(it, GROUPS * c)
                        if c > 0:
                            variance(it, c - 1)
                        if more:
                            project_w(it, c + 1)
                            project_tile(it, "k", WK, BK, c + 1)
                        else:
                            project_tile(it, "g", WG, BG, c)
                        reduce(it, GROUPS * c + 1)
                        uv_ready.wait(pe, it, c + 1)
                        nc.tensor.matmul(py[c % 2][:], cst[:, CENTRE], uv[:], start=False, stop=False)
                        if more:
                            project_tile(it, "r", WR, BR, c + 1)
                        reduce(it, GROUPS * c + 2)
                        if more:
                            project_tile(it, "v", WV, BV, c + 1)
                        reduce(it, GROUPS * c + 3)
                        if more:
                            project_tile(it, "g", WG, BG, c)
                    variance(it, CT - 1)
                    yg_ready.wait(pe, it, CT)
                    for t in range(TT):
                        project_tokens(it, ("wo", t), wf[:, WO], yg[:, :, 1:], t)
                    transposes(it, "xc", 1)
                    xk2_ready.wait(pe, it, CT)
                    for c in range(CT):
                        project(it, ("fk", c), wf[:, FK], xk2, P * c)
                    xr2_ready.wait(pe, it, CT)
                    for t in range(TT):
                        project_tokens(it, ("fr", t), wf[:, FR], xr2, t)
                    kk_ready.wait(pe, it, CT)
                    for t in range(TT):
                        project_tokens(it, ("fv", t), wf[:, FV], kk, t)


def program(nc):
    shapes = {
        "x": [B, T, C], "weights_a": [LAYERS, P, 4, CT, C], "weights_f": [LAYERS, P, 4, CT, C],
        "maa_w1": [LAYERS, P, CT, NF * DM], "maa_w2": [LAYERS, P, 2, C], "decay_w1": [LAYERS, P, CT, DD],
        "decay_w2": [LAYERS, DD, C], "vectors_a": [LAYERS, P, NVA, CT], "vectors_f": [LAYERS, P, NVF, CT],
        "prev": [P, B, 2, CT], "s0": [P, B, CT, S], "consts": [P, NCONST, P],
    }
    args = {n: nc.dram_tensor(f"in_{n}", s, F32, kind="ExternalInput").ap() for n, s in shapes.items()}
    out = nc.dram_tensor("out", [B, T, C], F32, kind="ExternalOutput").ap()
    build(nc, *args.values(), out)


def constants():
    row = np.arange(P)
    same = (row[:, None] // S == row[None, :] // S).astype(np.float32)
    m = np.zeros((P, NCONST, P), np.float32)
    m[:, IDENT] = np.eye(P)
    m[:, HMEAN] = same / S
    m[:, CENTRE] = np.eye(P) - same / S
    m[:, HONES] = same
    for v in range(S):
        m[:, REDUCE + v] = same * ((row % S == v)[None, :] - 1.0 / S)
    return m


def kernel(**inputs):
    import concourse.bacc as bacc
    from concourse.bass_utils import run_bass_kernel_spmd

    a = {k: np.asarray(v) for k, v in inputs.items()}

    def both(names0, names1, lay):
        return np.ascontiguousarray(np.stack([lay([a["L0_xattn_" + n] if isinstance(n, str) else n for n in names0]),
                                              lay([a["L1_xattn_" + n] if isinstance(n, str) else n for n in names1])]))

    def rows(w):
        return w.reshape(CT, P, -1).transpose(1, 0, 2)

    def transposed(ws):
        return np.stack([rows(w.T) for w in ws], axis=1)

    def columns(vs):
        return np.stack([v.reshape(CT, P).T for v in vs], axis=1)

    order0, order1 = [1, 0, 3, 2, 4], [0, 1, 3, 2, 4]
    stack = a["L0_xattn_maa_stack"]


    def maa_in(names, order):
        w = a[names].reshape(C, NF, DM)[:, order].reshape(C, NF * DM)
        return rows(w)

    def maa_out(names, order):
        w = a[names][order]
        return np.stack([w[:4].reshape(4 * DM, C), np.concatenate([w[4]] * 4)], axis=1)

    ctx = a["ctx_2048"]
    feeds = {
        "x": a["x"],
        "weights_a": both(["Wk", "Wr", "Wv", "Wg"], ["Wk", "Wr", "Wv", "Wg"], transposed),
        "weights_f": both(["Wo", "ffn_Wk", "ffn_Wr", "ffn_Wv"], ["Wo", "fWk", "fWr", "fWv"], transposed),
        "maa_w1": np.stack([maa_in("L0_xattn_maa_w1", order0), maa_in("L1_xattn_maa_w1", order1)]),
        "maa_w2": np.stack([maa_out("L0_xattn_maa_w2", order0), maa_out("L1_xattn_maa_w2", order1)]),
        "decay_w1": both(["decay_w1"], ["decay_w1"], lambda w: rows(w[0])),
        "decay_w2": both(["decay_w2"], ["decay_w2"], lambda w: w[0]),
        "vectors_a": both(["ln1_w", "ln1_b", "maa_x", stack[1], stack[0], stack[3], stack[2], stack[4], "time_decay", "faaaa"],
                          ["ln1_w", "ln1_b", "maa_x", "maa_w", "maa_k", "maa_r", "maa_v", "maa_g", "time_decay", "faaaa"], columns),
        "vectors_f": both(["gn_w", "gn_b", "ln2_w", "ln2_b", "ffn_maa_k", "ffn_maa_r"],
                          ["gn_w", "gn_b", "ln2_w", "ln2_b", "fmaa_k", "fmaa_r"], columns),
        "prev": ctx[:, :2].reshape(B, 2, CT, P).transpose(3, 0, 1, 2),
        "s0": ctx[:, 2:2 + S].reshape(B, CT, P, S).transpose(2, 0, 1, 3),
        "consts": constants(),
    }
    feeds = {f"in_{n}": np.ascontiguousarray(v) for n, v in feeds.items()}
    nc = bacc.Bacc("TRN2", target_bir_lowering=False, num_devices=1)
    program(nc)
    result = run_bass_kernel_spmd(nc, [feeds], core_ids=[0])
    return result.results[0]["out"]
```

```python
import numpy as np
import concourse.bass as bass
from concourse import mybir
from contextlib import ExitStack

F32 = mybir.dt.float32
ALU = mybir.AluOpType
ACT = mybir.ActivationFunctionType

P = 128
LAYERS, B, T, C = 2, 4, 512, 512
H, S = 32, 16
CT, TT = C // P, T // P
DM, DD, NF = 32, 64, 5
EPS = 1e-5
VG = 4
GROUPS = S // VG
SLOTS = 3
NGROUP = CT * GROUPS

BW, BK, BR, BV, BG = range(NF)
LN1W, LN1B, MAAX, MAAW, MAAK, MAAR, MAAV, MAAG, TDECAY, UBONUS = range(10)
NVA = 10
MAA = {BW: MAAW, BK: MAAK, BR: MAAR, BV: MAAV, BG: MAAG}
GNW, GNB, LN2W, LN2B, FMK, FMR = range(6)
NVF = 6
WK, WR, WV, WG = range(4)
WO, FK, FR, FV = range(4)
IDENT, HMEAN, CENTRE, HONES, REDUCE = 0, 1, 2, 3, 4
NCONST = REDUCE + S

WORK = 4
MIX_ORDER = [(f, c) for f in (BW, BV, BK, BR, BG) for c in range(CT)]


def mix_jobs(*branches):
    return [("mix", f, c) for f in branches for c in range(CT)]


JOBS = [("maa_hidden", 0), ("maa_hidden", 1)]
JOBS += mix_jobs(BW, BV) + [("decay_hidden",)] + mix_jobs(BK) + [("w", 0), ("v", 0)]
JOBS += mix_jobs(BR) + [("k", 0)] + mix_jobs(BG) + [("r", 0)]
for _c in range(1, CT):
    JOBS += [("w", _c), ("v", _c), ("k", _c), ("r", _c)] + [("g", _c - 2)] * (_c > 1)
JOBS += [("g", CT - 2), ("g", CT - 1)]
JOBS += [("wo", t) for t in range(TT)]
JOBS += [("xc", c) for c in range(CT)]
JOBS += [("fk", c) for c in range(CT)]
JOBS += [("fr", t) for t in range(TT)]
JOBS += [("xa", c) for c in range(CT)]
JOBS += [("fv", t) for t in range(TT)]
BANK = {job: i % WORK for i, job in enumerate(JOBS)}
TURN = {job: i // WORK for i, job in enumerate(JOBS)}
PER_BANK = [sum(BANK[j] == b for j in JOBS) for b in range(WORK)]


class Flag:

    def __init__(self, sem, per, primed=0):
        self.sem, self.per, self.primed = sem, per, primed

    def wait(self, engine, it, n):
        engine.wait_ge(self.sem, it * self.per + (n + self.primed))


def build(nc, x, weights_a, weights_f, maa_w1, maa_w2, decay_w1, decay_w2, vectors_a, vectors_f, prev, s0, consts, out):
    ctx = ExitStack()
    with ctx:
        def sb(name, shape):
            return ctx.enter_context(nc.sbuf_tensor(name, shape, F32))

        def flag(name, per=1, primed=0):
            return Flag(ctx.enter_context(nc.semaphore(name)), per, primed)

        wa = sb("wa", [P, 4, CT, C])
        wf = sb("wf", [P, 4, CT, C])
        mw1 = sb("mw1", [P, CT, NF * DM])
        mw2 = sb("mw2", [P, 2, C])
        dw1 = sb("dw1", [P, CT, DD])
        dw2 = sb("dw2", [DD, C])
        va = sb("va", [P, NVA, CT])
        vf = sb("vf", [P, NVF, CT])
        bonus = sb("bonus", [P, CT, P])
        cst = sb("cst", [P, NCONST, P])
        pv = sb("pv", [P, B, 2, CT])
        st0 = sb("st0", [P, B, CT, S])
        xres = sb("xres", [P, TT, C])
        xa = sb("xa", [P, CT, T + 1])
        sx = sb("sx", [P, CT, T])
        mixed = sb("mixed", [P, 4, CT, T])
        hid = sb("hid", [P, T])
        hid4 = sb("hid4", [DM, T])
        dhid = sb("dhid", [DD, T])
        kt = sb("kt", [P, 2, T])
        rt = sb("rt", [P, 2, T])
        vt = sb("vt", [P, 2, T])
        wt = sb("wt", [P, 2, T])
        ring = sb("ring", [P, SLOTS, VG, T])
        states = sb("states", [P, VG, T])
        rk = sb("rk", [P, T])
        uv = sb("uv", [P, T])
        sq = sb("sq", [P, T])
        yn = sb("yn", [P, T])
        stats = sb("stats", [P, TT, 6])
        mv = sb("mv", [P, TT, 2])
        vareps = sb("vareps", [P, TT])
        power = sb("power", [P, TT])
        rstd = sb("rstd", [P, TT])
        eps = sb("eps", [P, 1])
        srow = sb("srow", [P, CT, S])

        xn = ring[:, 1]
        normed = mixed[:, 0]
        xxx = mixed[:, 0]
        SLOT = {BK: 0, BR: 1, BV: 2, BW: 3, BG: 3}
        gate = sx
        yg = xa
        sig = mixed[:, 3]
        xk2, xr2, kk, rr = (mixed[:, i] for i in range(4))
        scratch = [rk, uv]

        work = [ctx.enter_context(nc.psum_tensor(f"work{i}", [P, 512], F32)) for i in range(WORK)]
        py = [ctx.enter_context(nc.psum_tensor(f"py{i}", [P, 512], F32)) for i in range(2)]
        pbonus = ctx.enter_context(nc.psum_tensor("pbonus", [P, 512], F32))
        pvar = ctx.enter_context(nc.psum_tensor("pvar", [P, 512], F32))

        first = [py[0], py[1], pbonus, pvar]

        full = [flag(f"work_full{b}", PER_BANK[b]) for b in range(WORK)]
        consts_in = flag("consts_in")
        gates_passed = flag("gates_passed")
        power_ready = flag("power_ready")
        vectors_a_in = flag("vectors_a_in")
        weights_a_in = flag("weights_a_in")
        weights_f_in = flag("weights_f_in")
        batch_done = flag("batch_done", TT, primed=1)
        bonus_ready = flag("bonus_ready")
        home = flag("home", 16)
        xn_in = flag("xn_in", 16)
        xres_in = flag("xres_in", 16)
        stats_done = flag("stats_done", 2 * TT)
        moments_done = flag("moments_done", 2 * TT)
        vareps_ready = flag("vareps_ready", 2)
        rstd_done = flag("rstd_done", 2)
        normed_ready = flag("normed_ready", 2 * TT)
        prev_ready = flag("prev_ready", 2)
        s0_ready = flag("s0_ready")
        xa_ready = flag("xa_ready", CT)
        sx_ready = flag("sx_ready", 2 * CT)
        xxx_ready = flag("xxx_ready", CT)
        hid_ready = flag("hid_ready", 2)
        dhid_ready = flag("dhid_ready")
        mterm_done = flag("mterm_done", NF * CT)
        mix_ready = flag("mix_ready", NF * CT)
        exp_done = flag("exp_done", CT)
        w_ready = flag("w_ready", CT)
        k_ready = flag("k_ready", CT)
        r_ready = flag("r_ready", CT)
        v_ready = flag("v_ready", CT)
        rk_ready = flag("rk_ready", CT)
        bonus_sum = flag("bonus_sum", CT)
        uv_ready = flag("uv_ready", CT)
        uses = [len(range(s, NGROUP, SLOTS)) for s in range(SLOTS)]
        vb_in = [flag(f"vb_in{s}", uses[s] * VG * 16) for s in range(SLOTS)]
        kv_done = flag("kv_done", NGROUP * 2)
        scan_done = flag("scan_done", NGROUP * VG)
        rs_ready = flag("rs_ready", NGROUP * 3)
        reduced = flag("reduced", NGROUP)
        sq_ready = flag("sq_ready", CT)
        var_ready = flag("var_ready", CT)
        yln_done = flag("yln_done", CT)
        ystd_done = flag("ystd_done", CT)
        yn_ready = flag("yn_ready", CT)
        affine_done = flag("affine_done", CT)
        gate_ready = flag("gate_ready", CT, primed=1)
        yz_done = flag("yz_done", CT)
        sig_ready = flag("sig_ready")
        yg_ready = flag("yg_ready", 3)
        xatt_ready = flag("xatt_ready", TT)
        xc_ready = flag("xc_ready", CT)
        xk2_ready = flag("xk2_ready", CT)
        xr2_ready = flag("xr2_ready", CT)
        relu_done = flag("relu_done", CT)
        kk_ready = flag("kk_ready", CT)
        rr_ready = flag("rr_ready", TT)
        gated_done = flag("gated_done", TT, primed=TT)
        first_turned = flag("first_turned")

        LEFT = {}
        for c in range(CT):
            LEFT["xa", c] = xa_ready, CT + c + 1
            LEFT["w", c] = exp_done, c + 1
            LEFT["k", c] = k_ready, c + 1
            LEFT["r", c] = r_ready, c + 1
            LEFT["v", c] = v_ready, c + 1
            LEFT["g", c] = gate_ready, c + 1
            LEFT["xc", c] = xc_ready, c + 1
            LEFT["fk", c] = relu_done, c + 1
        for t in range(TT):
            LEFT["wo", t] = xatt_ready, t + 1
            LEFT["fr", t] = rr_ready, t + 1
            LEFT["fv", t] = gated_done, t + 1
        for i in range(2):
            LEFT["maa_hidden", i] = hid_ready, i + 1
        for i, (f, c) in enumerate(MIX_ORDER):
            LEFT["mix", f, c] = mterm_done, i + 1
        LEFT["decay_hidden",] = dhid_ready, 1

        out_t = out.rearrange("b (i p) c -> b p i c", p=P)
        x_t = x.rearrange("b (i p) c -> b p i c", p=P)
        DMAS_A, DMAS_F = 4 + 4, 1 + 4

        def bank(job):
            return work[BANK[job]]

        def pass_gate(engine):
            engine.sem_inc(gates_passed.sem, 1)

        def take(engine, it, job):
            full[BANK[job]].wait(engine, it, TURN[job] + 1)

        def spread(c, v):
            rows = vt[:, c % 2]
            step = rows.ap[0][0]
            return bass.AP(rows.tensor, rows.offset + v * step, [[S * step, P // S], [0, S], [1, T]])

        block = ctx.enter_context(nc.Block())

        @block.sync
        def _(sp):
            for tile, src in ((cst, consts), (pv, prev), (st0, s0)):
                sp.dma_start(tile[:], src).then_inc(consts_in.sem, 16)
            sp.dma_start(va[:], vectors_a[0]).then_inc(vectors_a_in.sem, 16)
            with sp.Fori(0, LAYERS) as layer:
                gate_ready.wait(sp, layer * B, 0)
                pass_gate(sp)
                for tile, src in ((mw1, maa_w1), (mw2, maa_w2), (dw1, decay_w1), (dw2, decay_w2)):
                    sp.dma_start(tile[:], src[bass.ds(layer, 1)][0]).then_inc(weights_a_in.sem, 16)
                for i in (WV, WK, WR, WG):
                    sp.dma_start(wa[:, i], weights_a[bass.ds(layer, 1)][0, :, i]).then_inc(weights_a_in.sem, 16)
                batch_done.wait(sp, layer * B, 0)
                pass_gate(sp)
                sp.dma_start(vf[:], vectors_f[bass.ds(layer, 1)][0]).then_inc(weights_f_in.sem, 16)
                for i in range(4):
                    sp.dma_start(wf[:, i], weights_f[bass.ds(layer, 1)][0, :, i]).then_inc(weights_f_in.sem, 16)
                with sp.Fori(0, B) as b:
                    it = layer * B + b
                    for j in range(NGROUP):
                        c, q = j // GROUPS, j % GROUPS
                        if q == 0:
                            v_ready.wait(sp, it, c + 1)
                            pass_gate(sp)
                        if j >= SLOTS:
                            reduced.wait(sp, it, j - SLOTS + 1)
                        for i in range(VG):
                            sp.dma_start(ring[:, j % SLOTS, i], spread(c, VG * q + i)).then_inc(vb_in[j % SLOTS].sem, 16)
                gate_ready.wait(sp, layer * B + B, 0)
                pass_gate(sp)
                sp.dma_start(va[:], vectors_a[bass.ds((layer + 1) % LAYERS, 1)][0]).then_inc(vectors_a_in.sem, 16)
            sp.wait_ge(vectors_a_in.sem, 16 * (LAYERS + 1))

        @block.scalar
        def _(act):
            nc.scalar.nop().then_inc(gate_ready.sem, 1)
            act.dma_start(xn, x_t[0]).then_inc(xn_in.sem, 16)
            act.wait_ge(consts_in.sem, 3 * 16)
            act.wait_ge(power_ready.sem, 2)

            def leave(it, job, dst, func, done, **kw):
                take(act, it, job)
                nc.scalar.activation(dst, bank(job)[0:dst.shape[0], :], func, **kw).then_inc(done.sem, 1)

            def leave_w(it, c):
                leave(it, ("w", c), wt[:, c % 2], ACT.Exp, exp_done, bias=va[:, TDECAY, c:c + 1])
                exp_done.wait(act, it, c + 1)
                nc.scalar.activation(wt[:, c % 2], wt[:, c % 2], ACT.Exp, scale=-1.0).then_inc(w_ready.sem, 1)

            def leave_tile(it, name, c, dst, done):
                leave(it, (name, c), dst[:, c % 2], ACT.Identity, done)

            def square(it, c):
                reduced.wait(act, it, GROUPS * (c + 1))
                if c > 0:
                    var_ready.wait(act, it, c)
                nc.scalar.activation(sq[:], py[c % 2][:], ACT.Square).then_inc(sq_ready.sem, 1)

            def deviation(it, c):
                var_ready.wait(act, it, c + 1)
                if c > 0:
                    yz_done.wait(act, it, c)
                nc.scalar.activation(yn[:], pvar[:], ACT.Ln, bias=eps[:, 0:1]).then_inc(yln_done.sem, 1)
                yln_done.wait(act, it, c + 1)
                nc.scalar.activation(yn[:], yn[:], ACT.Exp, scale=-0.5).then_inc(ystd_done.sem, 1)

            def affine(it, c):
                yn_ready.wait(act, it, c + 1)
                nc.scalar.activation(yn[:], yn[:], ACT.Identity, scale=vf[:, GNW, c:c + 1],
                                     bias=vf[:, GNB, c:c + 1]).then_inc(affine_done.sem, 1)

            def xa_tiles(it, row, banks, full_of, ready, vectors, weight, bias):
                full_of(0)
                nc.scalar.copy(xa[:, :, 0], row).then_inc(prev_ready.sem, 1)
                for c in range(CT):
                    full_of(c)
                    nc.scalar.activation(xa[:, c, 1:], banks[c][:], ACT.Identity, scale=vectors[:, weight, c:c + 1],
                                         bias=vectors[:, bias, c:c + 1]).then_inc(ready.sem, 1)

            act.wait_ge(vectors_a_in.sem, 16)
            xa_tiles(0, pv[:, 0, 1], first, lambda c: act.wait_ge(first_turned.sem, c + 1), xa_ready, va, LN1W, LN1B)
            for b in range(B):
                act.dma_start(out[b], x[b]).then_inc(home.sem, 16)
            with act.Fori(0, LAYERS) as layer:
                with act.Fori(0, B) as b:
                    it = layer * B + b
                    nc.scalar.copy(srow[:], st0[:, bass.ds(b, 1)][:, 0]).then_inc(s0_ready.sem, 1)
                    leave(it, ("maa_hidden", 0), hid[:], ACT.Tanh, hid_ready)
                    leave(it, ("maa_hidden", 1), hid4[:], ACT.Tanh, hid_ready)
                    leave(it, ("decay_hidden",), dhid[:], ACT.Tanh, dhid_ready)
                    home.wait(act, it, 16 * B)
                    act.dma_start(xres[:], out_t[bass.ds(b, 1)][0]).then_inc(xres_in.sem, 16)
                    leave_w(it, 0)
                    leave_tile(it, "v", 0, vt, v_ready)
                    leave_tile(it, "k", 0, kt, k_ready)
                    leave_tile(it, "r", 0, rt, r_ready)
                    act.wait_ge(weights_f_in.sem, layer * (16 * DMAS_F) + 16 * DMAS_F)
                    for c in range(CT):
                        if c > 0:
                            square(it, c - 1)
                        if c < CT - 1:
                            if c > 0:
                                rs_ready.wait(act, it, 3 * GROUPS * c)
                            leave_w(it, c + 1)
                            leave_tile(it, "v", c + 1, vt, v_ready)
                        else:
                            leave(it, ("g", c - 1), gate[:, c - 1], ACT.Identity, gate_ready)
                        if c > 0:
                            deviation(it, c - 1)
                        if c < CT - 1:
                            leave_tile(it, "k", c + 1, kt, k_ready)
                        else:
                            leave(it, ("g", c), gate[:, c], ACT.Identity, gate_ready)
                            gate_ready.wait(act, it, CT)
                            nc.scalar.activation(sig, gate[:], ACT.Sigmoid).then_inc(sig_ready.sem, 1)
                        if c > 0:
                            affine(it, c - 1)
                        if c < CT - 1:
                            leave_tile(it, "r", c + 1, rt, r_ready)
                            if c > 0:
                                leave(it, ("g", c - 1), gate[:, c - 1], ACT.Identity, gate_ready)
                    square(it, CT - 1)
                    act.dma_start(xn, out_t[bass.ds((b + 1) % B, 1)][0]).then_inc(xn_in.sem, 16)
                    deviation(it, CT - 1)
                    affine(it, CT - 1)
                    xa_tiles(it, pv[:, bass.ds(b, 1)][:, 0, 0], [bank(("xc", c)) for c in range(CT)],
                             lambda c: take(act, it, ("xc", c)), xc_ready, vf, LN2W, LN2B)
                    for c in range(CT):
                        leave(it, ("fk", c), kk[:, c], ACT.Relu, relu_done)
                        relu_done.wait(act, it, c + 1)
                        nc.scalar.activation(kk[:, c], kk[:, c], ACT.Square).then_inc(kk_ready.sem, 1)
                    for t in range(TT):
                        leave(it, ("fr", t), rr[:, t], ACT.Sigmoid, rr_ready)
                    act.wait_ge(vectors_a_in.sem, (it + 1) // B * 16 + 16)
                    xr2_ready.wait(act, it, CT)
                    xa_tiles(it, pv[:, bass.ds((b + 1) % B, 1)][:, 0, 1], [bank(("xa", c)) for c in range(CT)],
                             lambda c: take(act, it, ("xa", c)), xa_ready, va, LN1W, LN1B)
                    batch_done.wait(act, it, TT)
                    act.dma_start(out_t[bass.ds(b, 1)][0], xres[:]).then_inc(home.sem, 16)
            act.wait_ge(home.sem, 16 * (B + LAYERS * B))
            act.wait_ge(xn_in.sem, 16 * (1 + LAYERS * B))

        @block.gpsimd
        def _(pool):
            nc.gpsimd.memset(power[:], -0.5).then_inc(power_ready.sem, 1)
            nc.gpsimd.memset(eps[:], EPS).then_inc(power_ready.sem, 1)
            pool.wait_ge(power_ready.sem, 2)
            with pool.Fori(0, 2 * LAYERS * B + 1) as i:
                pool.wait_ge(vareps_ready.sem, i + 1)
                nc.gpsimd.tensor_tensor(rstd[:], vareps[:], power[:], ALU.pow).then_inc(rstd_done.sem, 1)

        @block.vector
        def _(dve):
            nc.vector.nop().then_inc(batch_done.sem, 1)
            nc.vector.nop().then_inc(gated_done.sem, TT)
            dve.wait_ge(consts_in.sem, 3 * 16)

            def normalise(it, half, src, dst):
                n = half * TT
                for t in range(TT):
                    if half:
                        xatt_ready.wait(dve, it, t + 1)
                    nc.vector.bn_stats(stats[:, t], src[:, t]).then_inc(stats_done.sem, 1)
                stats_done.wait(dve, it, n + TT)
                pass_gate(dve)
                for t in range(TT):
                    nc.vector.bn_aggr(mv[:, t], stats[:, t]).then_inc(moments_done.sem, 1)
                moments_done.wait(dve, it, n + TT)
                nc.vector.tensor_scalar(vareps[:], mv[:, :, 1], EPS, None, ALU.add).then_inc(vareps_ready.sem, 1)
                rstd_done.wait(dve, it, half + 1)
                for t in range(TT):
                    nc.vector.tensor_scalar(dst[:, t], src[:, t], mv[:, t, 0:1], rstd[:, t:t + 1],
                                            ALU.subtract, ALU.mult).then_inc(normed_ready.sem, 1)

            def shift(it, half, c):
                nc.vector.tensor_tensor(sx[:, c], xa[:, c, 0:T], xa[:, c, 1:], ALU.subtract).then_inc(sx_ready.sem, 1)

            def blend(dst, c, weight, done):
                nc.vector.scalar_tensor_tensor(dst[:, c], sx[:, c], weight, xa[:, c, 1:], ALU.mult, ALU.add).then_inc(done.sem, 1)

            def shift_and_blend(it, half, dst, vectors, weight, done):
                for c in range(CT + 1):
                    if c < CT:
                        (xc_ready if half else xa_ready).wait(dve, it, c + 1)
                        shift(it, half, c)
                    if c > 0:
                        sx_ready.wait(dve, it, half * CT + c)
                        blend(dst, c - 1, vectors[:, weight, c - 1:c], done)

            def mix_add(it, i):
                f, c = MIX_ORDER[i]
                mterm_done.wait(dve, it, i + 1)
                nc.vector.tensor_tensor(mixed[:, SLOT[f], c], scratch[i % 2][:], xa[:, c, 1:],
                                        ALU.add).then_inc(mix_ready.sem, 1)

            def ynorm(it, c):
                ystd_done.wait(dve, it, c + 1)
                nc.vector.tensor_tensor(yn[:], py[c % 2][:], yn[:], ALU.mult).then_inc(yn_ready.sem, 1)

            def ygate(it, c):
                affine_done.wait(dve, it, c + 1)
                gate_ready.wait(dve, it, c + 1)
                nc.vector.tensor_tensor(yg[:, c, 1:], yn[:], gate[:, c], ALU.mult).then_inc(yz_done.sem, 1)

            def ysilu(it, lo, hi):
                if lo == 0:
                    sig_ready.wait(dve, it, 1)
                yz_done.wait(dve, it, hi)
                nc.vector.tensor_tensor(yg[:, lo:hi, 1:], yg[:, lo:hi, 1:], sig[:, lo:hi], ALU.mult).then_inc(yg_ready.sem, 1)

            def group(it, j):
                c, q = j // GROUPS, j % GROUPS
                s, h = j % SLOTS, c % 2
                vb_in[s].wait(dve, it, (j // SLOTS + 1) * VG * 16)
                for i in range(2):
                    part = ring[:, s, 2 * i:2 * i + 2]
                    nc.vector.tensor_tensor(part, part, kt[:, h:h + 1].broadcast_to([P, 2, T]),
                                            ALU.mult).then_inc(kv_done.sem, 1)
                if q == 0:
                    w_ready.wait(dve, it, c + 1)
                if j > 0:
                    rs_ready.wait(dve, it, 3 * j)
                for i in range(VG):
                    kv_done.wait(dve, it, 2 * j + i // 2 + 1)
                    nc.vector.tensor_tensor_scan(states[:, i], wt[:, h], ring[:, s, i],
                                                 srow[:, c, VG * q + i:VG * q + i + 1],
                                                 ALU.mult, ALU.add).then_inc(scan_done.sem, 1)
                for i in range(2):
                    scan_done.wait(dve, it, VG * j + 2 * i + 2)
                    nc.vector.tensor_tensor(ring[:, s, 2 * i:2 * i + 2, 1:], states[:, 2 * i:2 * i + 2, 0:T - 1],
                                            rt[:, h:h + 1, 1:].broadcast_to([P, 2, T - 1]),
                                            ALU.mult).then_inc(rs_ready.sem, 1)
                nc.vector.tensor_scalar(ring[:, s, :, 0], srow[:, c, VG * q:VG * q + VG], rt[:, h, 0:1], None,
                                        ALU.mult).then_inc(rs_ready.sem, 1)

            def first_half(it):
                xn_in.wait(dve, it, 16)
                normalise(it, 0, xn, xn)

            def second_half(it):
                prev_ready.wait(dve, it, 1)
                shift_and_blend(it, 0, xxx, va, MAAX, xxx_ready)

            first_half(0)
            second_half(0)
            with dve.Fori(0, LAYERS) as layer:
                for c in range(CT):
                    nc.vector.tensor_scalar(bonus[:, c], cst[:, HONES], va[:, UBONUS, c:c + 1], None,
                                            ALU.mult).then_inc(bonus_ready.sem, 1)
                with dve.Fori(0, B) as b:
                    it = layer * B + b
                    for i, (f, c) in enumerate(MIX_ORDER):
                        take(dve, it, ("mix", f, c))
                        if i >= 2:
                            mix_ready.wait(dve, it, i - 1)
                        if (f, c) == (BG, 0):
                            take(dve, it, ("decay_hidden",))
                        nc.vector.scalar_tensor_tensor(scratch[i % 2][:], bank(("mix", f, c))[:], va[:, MAA[f], c:c + 1],
                                                       sx[:, c], ALU.add, ALU.mult).then_inc(mterm_done.sem, 1)
                        if i > 0:
                            mix_add(it, i - 1)
                    mix_add(it, NF * CT - 1)
                    s0_ready.wait(dve, it, 1)
                    for c in range(CT):
                        k_ready.wait(dve, it, c + 1)
                        r_ready.wait(dve, it, c + 1)
                        v_ready.wait(dve, it, c + 1)
                        if c == 0:
                            mix_ready.wait(dve, it, NF * CT)
                        nc.vector.tensor_tensor(rk[:], rt[:, c % 2], kt[:, c % 2], ALU.mult).then_inc(rk_ready.sem, 1)
                        group(it, GROUPS * c)
                        bonus_sum.wait(dve, it, c + 1)
                        if c > 0:
                            reduced.wait(dve, it, GROUPS * c)
                        nc.vector.tensor_tensor(uv[:], pbonus[:], vt[:, c % 2], ALU.mult).then_inc(uv_ready.sem, 1)
                        group(it, GROUPS * c + 1)
                        group(it, GROUPS * c + 2)
                        if c > 0:
                            ynorm(it, c - 1)
                        if c == CT - 1:
                            ysilu(it, 0, CT - 2)
                        group(it, GROUPS * c + 3)
                        if c > 0:
                            ygate(it, c - 1)
                    ysilu(it, CT - 2, CT - 1)
                    ynorm(it, CT - 1)
                    ygate(it, CT - 1)
                    ysilu(it, CT - 1, CT)
                    xres_in.wait(dve, it, 16)
                    for t in range(TT):
                        take(dve, it, ("wo", t))
                        nc.vector.tensor_tensor(xres[:, t], bank(("wo", t))[:], xres[:, t], ALU.add).then_inc(xatt_ready.sem, 1)
                    normalise(it, 1, xres, normed)
                    prev_ready.wait(dve, it, 2)
                    dve.wait_ge(weights_f_in.sem, layer * (16 * DMAS_F) + 16 * DMAS_F)
                    shift_and_blend(it, 1, xk2, vf, FMK, xk2_ready)
                    for c in range(CT):
                        blend(xr2, c, vf[:, FMR, c:c + 1], xr2_ready)
                    first_half(it + 1)
                    dve.wait_ge(vectors_a_in.sem, (it + 1) // B * 16 + 16)
                    take(dve, it, ("fk", CT - 1))
                    second_half(it + 1)
                    for t in range(TT):
                        take(dve, it, ("fv", t))
                        rr_ready.wait(dve, it, t + 1)
                        if t >= 2:
                            batch_done.wait(dve, it, t - 1)
                        nc.vector.tensor_tensor(scratch[t % 2][:], bank(("fv", t))[:], rr[:, t], ALU.mult).then_inc(gated_done.sem, 1)
                        gated_done.wait(dve, it, t + 1)
                        nc.vector.tensor_tensor(xres[:, t], xres[:, t], scratch[t % 2][:], ALU.add).then_inc(batch_done.sem, 1)

        @block.tensor
        def _(pe):
            pe.wait_ge(consts_in.sem, 3 * 16)

            def enter(it, job):
                if TURN[job] > 0:
                    done, n = LEFT[JOBS[JOBS.index(job) - WORK]]
                    done.wait(pe, it, n)
                else:
                    name, t = [j for j in JOBS if BANK[j] == BANK[job]][-1]
                    assert name == "fv"
                    gated_done.wait(pe, it, t + 1 - TT)

            def filled(ins, job):
                ins.then_inc(full[BANK[job]].sem, 1)

            def project(it, job, weight, src, column, width=P, ready=None):
                enter(it, job)
                for i in range(CT):
                    if ready:
                        ready.wait(pe, it, i + 1)
                    ins = nc.tensor.matmul(bank(job)[0:width, :], weight[:, i, column:column + width], src[:, i],
                                           start=i == 0, stop=i == CT - 1)
                filled(ins, job)

            def project_tokens(it, job, weight, src, t, tiles=range(CT)):
                if tiles[0] == 0:
                    enter(it, job)
                for i in tiles:
                    ins = nc.tensor.matmul(bank(job)[:], src[:, i, P * t:P * (t + 1)], weight[:, i],
                                           start=i == 0, stop=i == CT - 1)
                if tiles[-1] == CT - 1:
                    filled(ins, job)

            def transposes(src, banks, before, after):
                for t in range(TT):
                    for c in range(CT):
                        before(t, c)
                        ins = nc.tensor.transpose(banks[c][:, P * t:P * (t + 1)], src[:, t, P * c:P * (c + 1)], cst[:, IDENT])
                        if t == TT - 1:
                            ins.then_inc(after(c), 1)

            def transpose_jobs(it, name, ready, src):
                def before(t, c):
                    if c == 0:
                        ready(t)
                    if t == 0:
                        enter(it, (name, c))

                transposes(src, [bank((name, c)) for c in range(CT)], before, lambda c: full[BANK[name, c]].sem)

            def mixes(it, f):
                for c in range(CT):
                    job = ("mix", f, c)
                    enter(it, job)
                    lo = DM * f if f < 4 else 0
                    src = hid if f < 4 else hid4
                    filled(nc.tensor.matmul(bank(job)[:], mw2[lo:lo + DM, f // 4, P * c:P * (c + 1)], src[lo:lo + DM, :],
                                            start=True, stop=True), job)

            def project_w(it, c):
                dhid_ready.wait(pe, it, 1)
                enter(it, ("w", c))
                filled(nc.tensor.matmul(bank(("w", c))[:], dw2[:, P * c:P * (c + 1)], dhid[:], start=True, stop=True), ("w", c))

            def project_tile(it, name, which, f, c):
                mix_ready.wait(pe, it, (MIX_ORDER.index((f, CT - 1)) + 1))
                project(it, (name, c), wa[:, which], mixed[:, SLOT[f]], P * c)

            def reduce(it, j):
                c, q = j // GROUPS, j % GROUPS
                if q == 0 and c >= 2:
                    yn_ready.wait(pe, it, c - 1)
                rs_ready.wait(pe, it, 3 * (j + 1))
                for i in range(VG):
                    ins = nc.tensor.matmul(py[c % 2][:], cst[:, REDUCE + VG * q + i], ring[:, j % SLOTS, i],
                                           start=q == 0 and i == 0, stop=q == GROUPS - 1 and i == VG - 1)
                ins.then_inc(reduced.sem, 1)

            def variance(it, c):
                sq_ready.wait(pe, it, c + 1)
                if c > 0:
                    yln_done.wait(pe, it, c)
                nc.tensor.matmul(pvar[:], cst[:, HMEAN], sq[:], start=True, stop=True).then_inc(var_ready.sem, 1)

            def recurrence_bonus(it, c):
                rk_ready.wait(pe, it, c + 1)
                if c > 0:
                    uv_ready.wait(pe, it, c)
                nc.tensor.matmul(pbonus[:], bonus[:, c], rk[:], start=True, stop=True).then_inc(bonus_sum.sem, 1)

            transposes(xn, first, lambda t, c: normed_ready.wait(pe, 0, t + 1) if c == 0 else None, lambda c: first_turned.sem)
            with pe.Fori(0, LAYERS) as layer:
                pe.wait_ge(weights_a_in.sem, layer * (16 * DMAS_A) + 16 * DMAS_A)
                pe.wait_ge(bonus_ready.sem, layer * CT + CT)
                pass_gate(pe)
                with pe.Fori(0, B) as b:
                    it = layer * B + b
                    xxx_ready.wait(pe, it, 1)
                    project(it, ("maa_hidden", 0), mw1, xxx, 0, ready=xxx_ready)
                    project(it, ("maa_hidden", 1), mw1, xxx, P, DM)
                    hid_ready.wait(pe, it, 2)
                    mixes(it, BW)
                    mixes(it, BV)
                    mix_ready.wait(pe, it, CT)
                    project(it, ("decay_hidden",), dw1, mixed[:, SLOT[BW]], 0, DD)
                    mixes(it, BK)
                    project_w(it, 0)
                    project_tile(it, "v", WV, BV, 0)
                    mixes(it, BR)
                    project_tile(it, "k", WK, BK, 0)
                    mixes(it, BG)
                    project_tile(it, "r", WR, BR, 0)
                    for c in range(CT):
                        more = c < CT - 1
                        recurrence_bonus(it, c)
                        reduce(it, GROUPS * c)
                        if c > 0:
                            variance(it, c - 1)
                        if more:
                            project_w(it, c + 1)
                            project_tile(it, "v", WV, BV, c + 1)
                        else:
                            project_tile(it, "g", WG, BG, c - 1)
                        reduce(it, GROUPS * c + 1)
                        uv_ready.wait(pe, it, c + 1)
                        nc.tensor.matmul(py[c % 2][:], cst[:, CENTRE], uv[:], start=False, stop=False)
                        if more:
                            project_tile(it, "k", WK, BK, c + 1)
                        else:
                            project_tile(it, "g", WG, BG, c)
                        reduce(it, GROUPS * c + 2)
                        if more:
                            project_tile(it, "r", WR, BR, c + 1)
                            if c > 0:
                                project_tile(it, "g", WG, BG, c - 1)
                        reduce(it, GROUPS * c + 3)
                    pe.wait_ge(weights_f_in.sem, layer * (16 * DMAS_F) + 16 * DMAS_F)
                    for tiles, n in ((range(CT - 2), 1), (range(CT - 2, CT - 1), 2), (range(CT - 1, CT), 3)):
                        yg_ready.wait(pe, it, n)
                        for t in range(TT):
                            project_tokens(it, ("wo", t), wf[:, WO], yg[:, :, 1:], t, tiles)
                            if n == 1 and t == 0:
                                variance(it, CT - 1)
                    transpose_jobs(it, "xc", lambda t: normed_ready.wait(pe, it, TT + t + 1), normed)
                    for c in range(CT):
                        project(it, ("fk", c), wf[:, FK], xk2, P * c, ready=xk2_ready if c == 0 else None)
                    xr2_ready.wait(pe, it, CT)
                    for t in range(TT):
                        project_tokens(it, ("fr", t), wf[:, FR], xr2, t)
                    transpose_jobs(it, "xa", lambda t: normed_ready.wait(pe, it + 1, t + 1), xn)
                    kk_ready.wait(pe, it, CT)
                    for t in range(TT):
                        project_tokens(it, ("fv", t), wf[:, FV], kk, t)


def program(nc):
    shapes = {
        "x": [B, T, C], "weights_a": [LAYERS, P, 4, CT, C], "weights_f": [LAYERS, P, 4, CT, C],
        "maa_w1": [LAYERS, P, CT, NF * DM], "maa_w2": [LAYERS, P, 2, C], "decay_w1": [LAYERS, P, CT, DD],
        "decay_w2": [LAYERS, DD, C], "vectors_a": [LAYERS, P, NVA, CT], "vectors_f": [LAYERS, P, NVF, CT],
        "prev": [P, B, 2, CT], "s0": [P, B, CT, S], "consts": [P, NCONST, P],
    }
    args = {n: nc.dram_tensor(f"in_{n}", s, F32, kind="ExternalInput").ap() for n, s in shapes.items()}
    out = nc.dram_tensor("out", [B, T, C], F32, kind="ExternalOutput").ap()
    build(nc, *args.values(), out)


def constants():
    row = np.arange(P)
    same = (row[:, None] // S == row[None, :] // S).astype(np.float32)
    m = np.zeros((P, NCONST, P), np.float32)
    m[:, IDENT] = np.eye(P)
    m[:, HMEAN] = same / S
    m[:, CENTRE] = np.eye(P) - same / S
    m[:, HONES] = same
    for v in range(S):
        m[:, REDUCE + v] = same * ((row % S == v)[None, :] - 1.0 / S)
    return m


def kernel(**inputs):
    import concourse.bacc as bacc
    from concourse.bass_utils import run_bass_kernel_spmd

    a = {k: np.asarray(v) for k, v in inputs.items()}

    def both(names0, names1, lay):
        return np.ascontiguousarray(np.stack([lay([a["L0_xattn_" + n] if isinstance(n, str) else n for n in names0]),
                                              lay([a["L1_xattn_" + n] if isinstance(n, str) else n for n in names1])]))

    def rows(w):
        return w.reshape(CT, P, -1).transpose(1, 0, 2)

    def transposed(ws):
        return np.stack([rows(w.T) for w in ws], axis=1)

    def columns(vs):
        return np.stack([v.reshape(CT, P).T for v in vs], axis=1)

    order0, order1 = [1, 0, 3, 2, 4], [0, 1, 3, 2, 4]
    stack = a["L0_xattn_maa_stack"]


    def maa_in(names, order):
        w = a[names].reshape(C, NF, DM)[:, order].reshape(C, NF * DM)
        return rows(w)

    def maa_out(names, order):
        w = a[names][order]
        return np.stack([w[:4].reshape(4 * DM, C), np.concatenate([w[4]] * 4)], axis=1)

    ctx = a["ctx_2048"]
    feeds = {
        "x": a["x"],
        "weights_a": both(["Wk", "Wr", "Wv", "Wg"], ["Wk", "Wr", "Wv", "Wg"], transposed),
        "weights_f": both(["Wo", "ffn_Wk", "ffn_Wr", "ffn_Wv"], ["Wo", "fWk", "fWr", "fWv"], transposed),
        "maa_w1": np.stack([maa_in("L0_xattn_maa_w1", order0), maa_in("L1_xattn_maa_w1", order1)]),
        "maa_w2": np.stack([maa_out("L0_xattn_maa_w2", order0), maa_out("L1_xattn_maa_w2", order1)]),
        "decay_w1": both(["decay_w1"], ["decay_w1"], lambda w: rows(w[0])),
        "decay_w2": both(["decay_w2"], ["decay_w2"], lambda w: w[0]),
        "vectors_a": both(["ln1_w", "ln1_b", "maa_x", stack[1], stack[0], stack[3], stack[2], stack[4], "time_decay", "faaaa"],
                          ["ln1_w", "ln1_b", "maa_x", "maa_w", "maa_k", "maa_r", "maa_v", "maa_g", "time_decay", "faaaa"], columns),
        "vectors_f": both(["gn_w", "gn_b", "ln2_w", "ln2_b", "ffn_maa_k", "ffn_maa_r"],
                          ["gn_w", "gn_b", "ln2_w", "ln2_b", "fmaa_k", "fmaa_r"], columns),
        "prev": ctx[:, :2].reshape(B, 2, CT, P).transpose(3, 0, 1, 2),
        "s0": ctx[:, 2:2 + S].reshape(B, CT, P, S).transpose(2, 0, 1, 3),
        "consts": constants(),
    }
    feeds = {f"in_{n}": np.ascontiguousarray(v) for n, v in feeds.items()}
    nc = bacc.Bacc("TRN2", target_bir_lowering=False, num_devices=1)
    program(nc)
    result = run_bass_kernel_spmd(nc, [feeds], core_ids=[0])
    return result.results[0]["out"]
```

```python
import numpy as np
import concourse.bass as bass
from concourse import mybir
from contextlib import ExitStack

F32 = mybir.dt.float32
ALU = mybir.AluOpType
ACT = mybir.ActivationFunctionType

P = 128
LAYERS, B, T, C = 2, 4, 512, 512
H, S = 32, 16
CT, TT = C // P, T // P
DM, DD, NF = 32, 64, 5
EPS = 1e-5
VG = 4
Q = P // VG
GROUPS = S // VG
SLOTS = 3
NGROUP = CT * GROUPS

BW, BK, BR, BV, BG = range(NF)
LN1W, LN1B, MAAX, MAAW, MAAK, MAAR, MAAV, MAAG, TDECAY, UBONUS = range(10)
NVA = 10
MAA = {BW: MAAW, BK: MAAK, BR: MAAR, BV: MAAV, BG: MAAG}
GNW, GNB, LN2W, LN2B, FMK, FMR = range(6)
NVF = 6
WK, WR, WV, WG = range(4)
WO, FK, FR, FV = range(4)
FSLOT = {WO: 0, FK: 1, FR: 0, FV: 1}
IDENT, HMEAN, CENTRE, HONES, REDUCE = range(5)
NCONST = 5

WORK = 4
JOBS = [("w", 1), ("v", 1), ("k", 1), ("r", 1), ("fk", 2), ("fk", 3)] + [("fr", t) for t in range(TT)]
JOBS += [("w", 2), ("v", 2), ("k", 2), ("r", 2), ("g", 0)]
JOBS += [("w", 3), ("v", 3), ("k", 3), ("r", 3), ("g", 1), ("g", 2), ("fv", 0), ("fv", 1), ("fv", 2), ("fv", 3), ("g", 3)]
JOBS += [("wo", t) for t in range(TT)] + [("w", 0)] + [("xc", c) for c in range(CT)]
JOBS += [("v", 0), ("k", 0), ("fk", 0), ("fk", 1), ("r", 0)]
FK_ORDER = [2, 3, 0, 1]
BANK = {job: i % WORK for i, job in enumerate(JOBS)}
TURN = {job: i // WORK for i, job in enumerate(JOBS)}
PER_BANK = [sum(BANK[j] == b for j in JOBS) for b in range(WORK)]
START = {("w", 0): 0, ("v", 0): 1, ("k", 0): 2, ("r", 0): 3}

MIX_ORDER = [(f, c) for f in (BW, BV, BK) for c in range(CT)] + [(f, c) for c in range(CT) for f in (BR, BG)]
MIXES = [("mix",) + fc for fc in MIX_ORDER]
SIDE = [("xa", c) for c in range(CT)] + [("maa_hidden",)] + MIXES[:CT + 3] + [("hidden2",)] + MIXES[CT + 3:]
SIDE_BANK = {job: i % 2 for i, job in enumerate(SIDE)}
SIDE_TURN = {job: i // 2 for i, job in enumerate(SIDE)}


class Flag:

    def __init__(self, sem, per, primed=0):
        self.sem, self.per, self.primed = sem, per, primed

    def at(self, it, n):
        return it * self.per + (n + self.primed)


def build(nc, x, weights_a, weights_f, maa_w1, maa_w2, decay_w1, decay_w2, vectors_a, vectors_f, prev, s0, consts, out):
    ctx = ExitStack()
    with ctx:
        def sb(name, shape):
            return ctx.enter_context(nc.sbuf_tensor(name, shape, F32))

        def flag(name, per=1, primed=0):
            return Flag(ctx.enter_context(nc.semaphore(name)), per, primed)

        wa = sb("wa", [P, 4, CT, C])
        wf = sb("wf", [P, 2, CT, C])
        mw1 = sb("mw1", [P, CT, NF * DM])
        mw2 = sb("mw2", [P, NF, C])
        dw1 = sb("dw1", [P, CT, DD])
        dw2 = sb("dw2", [P, C])
        va = sb("va", [P, NVA, CT])
        vf = sb("vf", [P, NVF, CT])
        bonus = sb("bonus", [P, CT, P])
        cst = sb("cst", [P, NCONST, P])
        pv = sb("pv", [P, B, 2, CT])
        st0 = sb("st0", [P, B, CT, S])
        xres = sb("xres", [P, TT, C])
        xa = sb("xa", [P, CT, T + 1])
        sx = sb("sx", [P, CT, T])
        ya = sb("ya", [P, CT, T + 1])
        gate = sb("gate", [P, CT, T])
        mix_k = sb("mix_k", [P, CT, T])
        mix_v = sb("mix_v", [P, CT, T])
        xr2 = sb("xr2", [P, CT, T])
        kk = sb("kk", [P, CT, T])
        hid = sb("hid", [P, T])
        hid2 = sb("hid2", [P, T])
        kt = sb("kt", [P, 2, T])
        rt = sb("rt", [P, 2, T])
        vt = sb("vt", [P, 2, T])
        wt = sb("wt", [P, 2, T])
        ring = sb("ring", [P, SLOTS, VG, T])
        states = sb("states", [P, VG, T + 1])
        rk = sb("rk", [P, T])
        uv = sb("uv", [P, T])
        sq = sb("sq", [P, T])
        yn = sb("yn", [P, T])
        stats = sb("stats", [P, 2, TT, 6])
        mv = sb("mv", [P, 2, TT, 2])
        vareps = sb("vareps", [P, 2, TT])
        power = sb("power", [P, TT])
        rstd = sb("rstd", [P, 2, TT])
        negmean = sb("negmean", [P, 2, TT])
        offset = sb("offset", [P, 2, TT])
        eps = sb("eps", [P, 1])
        srow = sb("srow", [P, CT, S])

        xn = mix_k
        xxx = mix_k
        mix_w = ring[:, 2]
        mix_r = xa[:, :, 1:]
        mix_g = sx
        MIXED = {BW: mix_w, BV: mix_v, BK: mix_k, BR: mix_r, BG: mix_g}
        yg = ya[:, :, 1:]
        normed = ring[:, 1]
        xc = ya
        sxc = states[:, :, 1:]
        xk2 = gate
        rr = xr2
        scratch = [rk[:], rt[:, 0]]

        work = [ctx.enter_context(nc.psum_tensor(f"work{i}", [P, 512], F32)) for i in range(WORK)]
        py = [ctx.enter_context(nc.psum_tensor(f"py{i}", [P, 512], F32)) for i in range(2)]
        pbonus = ctx.enter_context(nc.psum_tensor("pbonus", [P, 512], F32))
        pvar = ctx.enter_context(nc.psum_tensor("pvar", [P, 512], F32))

        side = [py[0], pbonus]

        full = [flag(f"work_full{b}", PER_BANK[b], primed=1) for b in range(WORK)]
        side_full = [flag(f"side_full{b}", len(SIDE) // 2) for b in range(2)]
        consts_in = flag("consts_in")
        gates_passed = flag("gates_passed")
        power_ready = flag("power_ready")
        zeros_ready = flag("zeros_ready")
        small_in = flag("small_in", 5 * 16)
        weights_a_in = flag("weights_a_in", 4 * 16)
        vectors_f_in = flag("vectors_f_in", 16)
        slot_in = [flag(f"wf_in{i}", 2 * 16, primed=16 * i) for i in range(2)]
        batch_done = flag("batch_done", TT)
        bonus_ready = flag("bonus_ready")
        home = flag("home", 16)
        xn_in = flag("xn_in", 16)
        xres_in = flag("xres_in", 16, primed=16)
        stats_done = [flag(f"stats_done{i}", TT) for i in range(2)]
        moments_done = [flag(f"moments_done{i}", TT) for i in range(2)]
        vareps_ready = [flag(f"vareps_ready{i}", 2) for i in range(2)]
        rstd_done = [flag(f"rstd_done{i}") for i in range(2)]
        offset_ready = [flag(f"offset_ready{i}") for i in range(2)]
        normed_ready = [flag(f"normed_ready{i}", TT) for i in range(2)]
        prev_ready = [flag(f"prev_ready{i}") for i in range(2)]
        s0_ready = flag("s0_ready")
        xa_ready = flag("xa_ready", CT)
        sx_ready = [flag(f"sx_ready{i}", CT) for i in range(2)]
        xxx_ready = flag("xxx_ready", CT)
        hid_ready = flag("hid_ready")
        hid2_ready = flag("hid2_ready")
        mterm_done = flag("mterm_done", NF * CT)
        mix_ready = flag("mix_ready", NF * CT)
        exp_done = flag("exp_done", CT)
        w_ready = flag("w_ready", CT)
        k_ready = flag("k_ready", CT)
        r_ready = flag("r_ready", CT)
        v_ready = flag("v_ready", CT)
        rk_ready = flag("rk_ready", CT)
        bonus_sum = flag("bonus_sum", CT)
        uv_ready = flag("uv_ready", CT)
        uses = [len(range(s, NGROUP, SLOTS)) for s in range(SLOTS)]
        vb_in = [flag(f"vb_in{s}", uses[s] * VG * 16) for s in range(SLOTS)]
        kv_done = flag("kv_done", NGROUP * 2)
        scan_done = flag("scan_done", NGROUP * VG)
        rs_ready = flag("rs_ready", NGROUP * 2, primed=1)
        column_ready = flag("column_ready", NGROUP)
        reduced = flag("reduced", NGROUP)
        raw_ready = flag("raw_ready", CT)
        centred = flag("centred", CT)
        sq_ready = flag("sq_ready", CT)
        var_ready = flag("var_ready", CT)
        yln_done = flag("yln_done", CT)
        ystd_done = flag("ystd_done", CT)
        yn_ready = flag("yn_ready", CT)
        affine_done = flag("affine_done", CT)
        gate_ready = flag("gate_ready", CT, primed=1)
        yg_ready = flag("yg_ready", CT)
        xatt_ready = flag("xatt_ready", TT, primed=1)
        xc_ready = flag("xc_ready", CT, primed=1)
        xk2_ready = flag("xk2_ready", CT, primed=1)
        xr2_ready = flag("xr2_ready", CT, primed=1)
        relu_done = flag("relu_done", CT, primed=CT)
        kk_ready = flag("kk_ready", CT, primed=1)
        rr_ready = flag("rr_ready", TT)
        gated_done = flag("gated_done", TT)
        last = [py[0], py[1], pbonus, pvar]
        last_fr = flag("last_fr", TT)
        last_fk = flag("last_fk", 2)
        last_fv = flag("last_fv", TT)

        LEFT = {}
        for c in range(CT):
            ahead = CT if c == 0 else 0
            LEFT["w", c] = exp_done, ahead + c + 1
            LEFT["k", c] = k_ready, ahead + c + 1
            LEFT["r", c] = r_ready, ahead + c + 1
            LEFT["v", c] = v_ready, ahead + c + 1
            LEFT["g", c] = gate_ready, c + 1
            LEFT["xc", c] = xc_ready, c + 1
            LEFT["fk", c] = relu_done, FK_ORDER.index(c) + 1
            LEFT["xa", c] = xa_ready, c + 1
        for t in range(TT):
            LEFT["wo", t] = xatt_ready, t + 1
            LEFT["fr", t] = rr_ready, t + 1
            LEFT["fv", t] = gated_done, t + 1
        for i, job in enumerate(MIXES):
            LEFT[job] = mterm_done, i + 1
        LEFT["maa_hidden",] = hid_ready, 1
        LEFT["hidden2",] = hid2_ready, 1

        out_t = out.rearrange("b (i p) c -> b p i c", p=P)
        x_t = x.rearrange("b (i p) c -> b p i c", p=P)

        def bank(it, job):
            return work[START[job] if it is None else BANK[job]]

        def side_bank(job):
            return side[SIDE_BANK[job]]

        def pass_gate(engine):
            engine.sem_inc(gates_passed.sem, 1)

        def take(engine, it, job):
            if it is None:
                engine.wait_ge(full[START[job]].sem, 1)
            else:
                engine.wait_ge(full[BANK[job]].sem, full[BANK[job]].at(it, TURN[job] + 1))

        def take_side(engine, of, job):
            flag = side_full[SIDE_BANK[job]]
            engine.wait_ge(flag.sem, flag.at(of, SIDE_TURN[job] + 1))

        def spread(c, v):
            rows = vt[:, c % 2]
            step = rows.ap[0][0]
            return bass.AP(rows.tensor, rows.offset + (Q * (v % VG) + v // VG) * step, [[GROUPS * step, P // S], [0, S], [1, T]])

        block = ctx.enter_context(nc.Block())

        @block.sync
        def _(sp):
            def load_attention(layer):
                layers = bass.ds(layer % LAYERS, 1)
                sp.dma_start(va[:], vectors_a[layers][0]).then_inc(small_in.sem, 16)
                sp.dma_start(mw1[:], maa_w1[layers][0]).then_inc(small_in.sem, 16)
                sp.dma_start(dw1[:], decay_w1[layers][0]).then_inc(small_in.sem, 16)
                sp.dma_start(dw2[:], decay_w2[layers][0]).then_inc(small_in.sem, 16)
                sp.dma_start(mw2[:], maa_w2[layers][0]).then_inc(small_in.sem, 16)
                for i in (WV, WK, WR, WG):
                    sp.dma_start(wa[:, i], weights_a[layers][0, :, i]).then_inc(weights_a_in.sem, 16)

            def load_f(layer, which):
                slot = FSLOT[which]
                sp.dma_start(wf[:, slot], weights_f[bass.ds(layer, 1)][0, :, which]).then_inc(slot_in[slot].sem, 16)

            for tile, src in ((cst, consts), (pv, prev), (st0, s0)):
                sp.dma_start(tile[:], src).then_inc(consts_in.sem, 16)
            load_attention(0)
            load_f(0, FK)
            with sp.Fori(0, LAYERS) as layer:
                with sp.Fori(0, B) as b:
                    it = layer * B + b
                    before = (it + (LAYERS * B - 1)) // B % LAYERS
                    sp.wait_ge(xatt_ready.sem, xatt_ready.at(it, 0))
                    pass_gate(sp)
                    load_f(before, FR)
                    for j in range(NGROUP):
                        c, q = j // GROUPS, j % GROUPS
                        if q == 0:
                            sp.wait_ge(v_ready.sem, v_ready.at(it, c + 1))
                            pass_gate(sp)
                        if j == 1:
                            sp.wait_ge(xc_ready.sem, xc_ready.at(it, 0))
                            pass_gate(sp)
                        if j == SLOTS:
                            sp.wait_ge(xr2_ready.sem, xr2_ready.at(it, 0))
                            pass_gate(sp)
                            sp.dma_start(vf[:], vectors_f[bass.ds(layer, 1)][0]).then_inc(vectors_f_in.sem, 16)
                        if j == GROUPS + 3:
                            sp.wait_ge(relu_done.sem, relu_done.at(it, 2))
                            pass_gate(sp)
                            load_f(before, FV)
                        if j == 2 * GROUPS + 1:
                            take(sp, it, ("fr", TT - 1))
                            pass_gate(sp)
                            load_f(layer, WO)
                        if j >= SLOTS:
                            sp.wait_ge(reduced.sem, reduced.at(it, j - SLOTS + 1))
                        for i in range(VG):
                            sp.dma_start(ring[:, j % SLOTS, i], spread(c, VG * q + i)).then_inc(vb_in[j % SLOTS].sem, 16)
                    take(sp, it, ("fv", TT - 1))
                    pass_gate(sp)
                    load_f(layer, FK)
                sp.wait_ge(gate_ready.sem, gate_ready.at(layer * B + (B - 1), CT))
                pass_gate(sp)
                load_attention(layer + 1)
            sp.wait_ge(xatt_ready.sem, xatt_ready.at(LAYERS * B, 0))
            load_f(LAYERS - 1, FR)
            sp.wait_ge(relu_done.sem, relu_done.at(LAYERS * B, 2))
            load_f(LAYERS - 1, FV)
            sp.wait_ge(weights_a_in.sem, weights_a_in.at(LAYERS, 4 * 16))
            sp.wait_ge(small_in.sem, small_in.at(LAYERS, 5 * 16))

        @block.scalar
        def _(act):
            nc.scalar.nop().then_inc(gate_ready.sem, 1)
            nc.scalar.nop().then_inc(xc_ready.sem, 1)
            nc.scalar.nop().then_inc(relu_done.sem, CT)
            act.dma_start(xn[:], x_t[0]).then_inc(xn_in.sem, 16)
            act.wait_ge(consts_in.sem, 3 * 16)
            act.wait_ge(power_ready.sem, 2)

            def leave(it, job, dst, func, done, **kw):
                take(act, it, job)
                nc.scalar.activation(dst, bank(it, job)[:], func, **kw).then_inc(done.sem, 1)

            def leave_w(it, of, c):
                leave(it, ("w", c), wt[:, c % 2], ACT.Exp, exp_done, bias=va[:, TDECAY, c:c + 1])
                act.wait_ge(exp_done.sem, exp_done.at(of, c + 1))
                nc.scalar.activation(wt[:, c % 2], wt[:, c % 2], ACT.Exp, scale=-1.0).then_inc(w_ready.sem, 1)

            def leave_tile(it, name, c, dst, done):
                leave(it, (name, c), dst[:, c % 2], ACT.Identity, done)

            def leave_gate(it, c):
                leave(it, ("g", c), gate[:, c], ACT.Silu, gate_ready)

            def normalise(it, half, src, dst):
                act.wait_ge(offset_ready[half].sem, offset_ready[half].at(it, 1))
                for t in range(TT):
                    nc.scalar.activation(dst[:, t], src[:, t], ACT.Identity, scale=rstd[:, half, t:t + 1],
                                         bias=offset[:, half, t:t + 1]).then_inc(normed_ready[half].sem, 1)

            def receptance(it):
                for t in range(TT):
                    nc.scalar.activation(rr[:, t], (work[BANK["fr", t]] if it is not None else last[t])[:],
                                         ACT.Sigmoid).then_inc(rr_ready.sem, 1)

            def ffn_key(it, c):
                if it is None:
                    it = LAYERS * B
                    act.wait_ge(last_fk.sem, c - 1)
                    nc.scalar.activation(kk[:, c], work[c - 2][:], ACT.Relu).then_inc(relu_done.sem, 1)
                else:
                    leave(it, ("fk", c), kk[:, c], ACT.Relu, relu_done)
                act.wait_ge(relu_done.sem, relu_done.at(it, FK_ORDER.index(c) + 1))
                nc.scalar.activation(kk[:, c], kk[:, c], ACT.Square).then_inc(kk_ready.sem, 1)

            def raw(it, c):
                act.wait_ge(reduced.sem, reduced.at(it, GROUPS * (c + 1)))
                if c > 0:
                    act.wait_ge(var_ready.sem, var_ready.at(it, c))
                nc.scalar.activation(sq[:], py[c % 2][:], ACT.Identity).then_inc(raw_ready.sem, 1)

            def square(it, c):
                act.wait_ge(centred.sem, centred.at(it, c + 1))
                nc.scalar.activation(sq[:], py[c % 2][:], ACT.Square).then_inc(sq_ready.sem, 1)

            def deviation(it, c):
                act.wait_ge(var_ready.sem, var_ready.at(it, c + 1))
                if c > 0:
                    act.wait_ge(yg_ready.sem, yg_ready.at(it, c))
                nc.scalar.activation(yn[:], pvar[:], ACT.Ln, bias=eps[:, 0:1]).then_inc(yln_done.sem, 1)
                act.wait_ge(yln_done.sem, yln_done.at(it, c + 1))
                nc.scalar.activation(yn[:], yn[:], ACT.Exp, scale=-0.5).then_inc(ystd_done.sem, 1)

            def affine(it, c):
                act.wait_ge(yn_ready.sem, yn_ready.at(it, c + 1))
                nc.scalar.activation(yn[:], yn[:], ACT.Identity, scale=vf[:, GNW, c:c + 1],
                                     bias=vf[:, GNB, c:c + 1]).then_inc(affine_done.sem, 1)

            def normed_tile(dst, c, source, ready, vectors, weight, bias):
                nc.scalar.activation(dst[:, c, 1:], source[:], ACT.Identity, scale=vectors[:, weight, c:c + 1],
                                     bias=vectors[:, bias, c:c + 1]).then_inc(ready.sem, 1)

            def attention_tiles(of, row):
                act.wait_ge(small_in.sem, small_in.at(of // B, 5 * 16))
                nc.scalar.copy(xa[:, :, 0], row).then_inc(prev_ready[0].sem, 1)
                for c in range(CT):
                    take_side(act, of, ("xa", c))
                    normed_tile(xa, c, side_bank(("xa", c)), xa_ready, va, LN1W, LN1B)

            def hidden(of):
                take_side(act, of, ("maa_hidden",))
                nc.scalar.activation(hid[:], side_bank(("maa_hidden",))[:], ACT.Tanh).then_inc(hid_ready.sem, 1)

            def hidden2(of):
                take_side(act, of, ("hidden2",))
                nc.scalar.activation(hid2[0:DD + DM], side_bank(("hidden2",))[0:DD + DM, :], ACT.Tanh).then_inc(hid2_ready.sem, 1)

            nc.scalar.copy(srow[:], st0[:, 0]).then_inc(s0_ready.sem, 1)
            normalise(0, 0, xn, xn)
            attention_tiles(0, pv[:, 0, 1])
            act.dma_start(xres[:], x_t[B - 1]).then_inc(xres_in.sem, 16)
            for b in range(B - 1):
                act.dma_start(out[b], x[b]).then_inc(home.sem, 16)
            hidden(0)
            hidden2(0)
            leave_w(None, 0, 0)
            leave_tile(None, "v", 0, vt, v_ready)
            leave_tile(None, "k", 0, kt, k_ready)
            leave_tile(None, "r", 0, rt, r_ready)
            act.wait_ge(home.sem, 16 * (B - 1))
            with act.Fori(0, LAYERS) as layer:
                with act.Fori(0, B) as b:
                    it = layer * B + b
                    leave_w(it, it, 1)
                    leave_tile(it, "v", 1, vt, v_ready)
                    leave_tile(it, "k", 1, kt, k_ready)
                    ffn_key(it, 2)
                    leave_tile(it, "r", 1, rt, r_ready)
                    ffn_key(it, 3)
                    raw(it, 0)
                    square(it, 0)
                    deviation(it, 0)
                    take(act, it, ("fr", TT - 1))
                    receptance(it)
                    act.wait_ge(rs_ready.sem, rs_ready.at(it, 2 * GROUPS))
                    leave_w(it, it, 2)
                    leave_tile(it, "v", 2, vt, v_ready)
                    leave_tile(it, "k", 2, kt, k_ready)
                    act.wait_ge(vectors_f_in.sem, vectors_f_in.at(it, 16))
                    affine(it, 0)
                    leave_tile(it, "r", 2, rt, r_ready)
                    leave_gate(it, 0)
                    raw(it, 1)
                    act.wait_ge(rs_ready.sem, rs_ready.at(it, 2 * 2 * GROUPS))
                    leave_w(it, it, 3)
                    square(it, 1)
                    leave_tile(it, "v", 3, vt, v_ready)
                    deviation(it, 1)
                    leave_tile(it, "k", 3, kt, k_ready)
                    act.dma_start(xn[:], out_t[bass.ds((b + 1) % B, 1)][0]).then_inc(xn_in.sem, 16)
                    affine(it, 1)
                    leave_tile(it, "r", 3, rt, r_ready)
                    leave_gate(it, 1)
                    leave_gate(it, 2)
                    raw(it, 2)
                    square(it, 2)
                    normalise(it + 1, 0, xn, xn)
                    deviation(it, 2)
                    affine(it, 2)
                    leave_gate(it, CT - 1)
                    attention_tiles(it + 1, pv[:, bass.ds((b + 1) % B, 1)][:, 0, 1])
                    act.wait_ge(batch_done.sem, batch_done.at(it, TT))
                    act.dma_start(out_t[bass.ds((b + (B - 1)) % B, 1)][0], xres[:]).then_inc(home.sem, 16)
                    hidden(it + 1)
                    raw(it, CT - 1)
                    square(it, CT - 1)
                    act.wait_ge(home.sem, home.at(it, 16 * B))
                    act.dma_start(xres[:], out_t[bass.ds(b, 1)][0]).then_inc(xres_in.sem, 16)
                    deviation(it, CT - 1)
                    affine(it, CT - 1)
                    hidden2(it + 1)
                    leave_w(it, it + 1, 0)
                    act.wait_ge(rs_ready.sem, rs_ready.at(it, 2 * NGROUP))
                    nc.scalar.copy(srow[:], st0[:, bass.ds((b + 1) % B, 1)][:, 0]).then_inc(s0_ready.sem, 1)
                    normalise(it, 1, xres, normed)
                    take(act, it, ("xc", 0))
                    nc.scalar.copy(xc[:, :, 0], pv[:, bass.ds(b, 1)][:, 0, 0]).then_inc(prev_ready[1].sem, 1)
                    for c in range(CT):
                        take(act, it, ("xc", c))
                        normed_tile(xc, c, bank(it, ("xc", c)), xc_ready, vf, LN2W, LN2B)
                    leave_tile(it, "v", 0, vt, v_ready)
                    leave_tile(it, "k", 0, kt, k_ready)
                    ffn_key(it, 0)
                    ffn_key(it, 1)
                    leave_tile(it, "r", 0, rt, r_ready)
            ffn_key(None, 2)
            ffn_key(None, 3)
            act.wait_ge(last_fr.sem, TT)
            receptance(None)
            for t in range(TT):
                act.wait_ge(batch_done.sem, batch_done.at(LAYERS * B, t + 1))
                act.dma_start(out_t[B - 1, :, t], xres[:, t]).then_inc(home.sem, 16)
            act.wait_ge(home.sem, 16 * (B - 1 + LAYERS * B + TT))
            act.wait_ge(xn_in.sem, 16 * (1 + LAYERS * B))

        @block.gpsimd
        def _(pool):
            nc.gpsimd.memset(power[:], -0.5).then_inc(power_ready.sem, 1)
            nc.gpsimd.memset(eps[:], EPS).then_inc(power_ready.sem, 1)
            pool.wait_ge(power_ready.sem, 2)

            def root(it, half):
                pool.wait_ge(vareps_ready[half].sem, vareps_ready[half].at(it, 2))
                nc.gpsimd.tensor_tensor(rstd[:, half], vareps[:, half], power[:], ALU.pow).then_inc(rstd_done[half].sem, 1)
                pool.wait_ge(rstd_done[half].sem, rstd_done[half].at(it, 1))
                nc.gpsimd.tensor_tensor(offset[:, half], negmean[:, half], rstd[:, half], ALU.mult).then_inc(offset_ready[half].sem, 1)

            def column(it, j):
                c, q = j // GROUPS, j % GROUPS
                if j == 0:
                    pool.wait_ge(s0_ready.sem, s0_ready.at(it, 1))
                pool.wait_ge(rs_ready.sem, rs_ready.at(it, 2 * j))
                pass_gate(pool)
                nc.gpsimd.tensor_copy(states[:, :, 0], srow[:, c, VG * q:VG * q + VG]).then_inc(column_ready.sem, 1)

            root(0, 0)
            with pool.Fori(0, LAYERS * B) as it:
                for j in range(3 * GROUPS + 1):
                    column(it, j)
                root(it + 1, 0)
                for j in range(3 * GROUPS + 1, NGROUP):
                    column(it, j)
                root(it, 1)

        @block.vector
        def _(dve):
            nc.vector.nop().then_inc(xatt_ready.sem, 1)
            nc.vector.nop().then_inc(rs_ready.sem, 1)
            dve.wait_ge(consts_in.sem, 3 * 16)

            def moments(it, half):
                dve.wait_ge(stats_done[half].sem, stats_done[half].at(it, TT))
                pass_gate(dve)
                for t in range(TT):
                    nc.vector.bn_aggr(mv[:, half, t], stats[:, half, t]).then_inc(moments_done[half].sem, 1)
                dve.wait_ge(moments_done[half].sem, moments_done[half].at(it, TT))
                nc.vector.tensor_scalar(vareps[:, half], mv[:, half, :, 1], EPS, None, ALU.add).then_inc(vareps_ready[half].sem, 1)
                nc.vector.tensor_scalar(negmean[:, half], mv[:, half, :, 0], -1.0, None, ALU.mult).then_inc(vareps_ready[half].sem, 1)

            def shift_and_blend(it, half, src, shifted, ready, dst, vectors, weight, done):
                dve.wait_ge(prev_ready[half].sem, prev_ready[half].at(it, 1))
                for c in range(CT + 1):
                    if c < CT:
                        dve.wait_ge(ready.sem, ready.at(it, c + 1))
                        nc.vector.tensor_tensor(shifted[:, c], src[:, c, 0:T], src[:, c, 1:], ALU.subtract).then_inc(sx_ready[half].sem, 1)
                    if c > 0:
                        dve.wait_ge(sx_ready[half].sem, sx_ready[half].at(it, c))
                        blend(dst, src, shifted, c - 1, vectors[:, weight, c - 1:c], done)

            def blend(dst, src, shifted, c, weight, done):
                nc.vector.scalar_tensor_tensor(dst[:, c], shifted[:, c], weight, src[:, c, 1:], ALU.mult, ALU.add).then_inc(done.sem, 1)

            def mix_term(of, i, free):
                f, c = MIX_ORDER[i]
                take_side(dve, of, MIXES[i])
                if free > 0:
                    dve.wait_ge(mix_ready.sem, mix_ready.at(of, free))
                nc.vector.scalar_tensor_tensor(scratch[i % 2], side_bank(MIXES[i])[:], va[:, MAA[f], c:c + 1], sx[:, c],
                                               ALU.add, ALU.mult).then_inc(mterm_done.sem, 1)

            def mix_add(of, i):
                f, c = MIX_ORDER[i]
                dve.wait_ge(mterm_done.sem, mterm_done.at(of, i + 1))
                nc.vector.tensor_tensor(MIXED[f][:, c], scratch[i % 2], xa[:, c, 1:], ALU.add).then_inc(mix_ready.sem, 1)

            def mix(of, lo, hi):
                for i in range(lo, hi):
                    mix_term(of, i, i - 1)
                    if i > lo:
                        mix_add(of, i - 1)
                mix_add(of, hi - 1)

            def mix_pair(of, c):
                i = MIX_ORDER.index((BR, c))
                mix_term(of, i, i)
                mix_term(of, i + 1, i)
                dve.wait_ge(mterm_done.sem, mterm_done.at(of, i + 2))
                mix_add(of, i + 1)
                mix_add(of, i)

            def ynorm(it, c):
                dve.wait_ge(ystd_done.sem, ystd_done.at(it, c + 1))
                nc.vector.tensor_tensor(yn[:], py[c % 2][:], yn[:], ALU.mult).then_inc(yn_ready.sem, 1)

            def ygate(it, c):
                dve.wait_ge(affine_done.sem, affine_done.at(it, c + 1))
                dve.wait_ge(gate_ready.sem, gate_ready.at(it, c + 1))
                nc.vector.tensor_tensor(yg[:, c], yn[:], gate[:, c], ALU.mult).then_inc(yg_ready.sem, 1)

            def group(it, j):
                c, q = j // GROUPS, j % GROUPS
                s, h = j % SLOTS, c % 2
                if q == 0:
                    dve.wait_ge(k_ready.sem, k_ready.at(it, c + 1))
                dve.wait_ge(vb_in[s].sem, vb_in[s].at(it, (j // SLOTS + 1) * VG * 16))
                for i in range(2):
                    part = ring[:, s, 2 * i:2 * i + 2]
                    nc.vector.tensor_tensor(part, part, kt[:, h:h + 1].broadcast_to([P, 2, T]),
                                            ALU.mult).then_inc(kv_done.sem, 1)
                if q == 0:
                    dve.wait_ge(w_ready.sem, w_ready.at(it, c + 1))
                if j > 0:
                    dve.wait_ge(rs_ready.sem, rs_ready.at(it, 2 * j))
                for i in range(VG):
                    dve.wait_ge(kv_done.sem, kv_done.at(it, 2 * j + i // 2 + 1))
                    nc.vector.tensor_tensor_scan(states[:, i, 1:], wt[:, h], ring[:, s, i],
                                                 srow[:, c, VG * q + i:VG * q + i + 1],
                                                 ALU.mult, ALU.add).then_inc(scan_done.sem, 1)
                if q == 0:
                    dve.wait_ge(r_ready.sem, r_ready.at(it, c + 1))
                    nc.vector.tensor_tensor(rk[:], rt[:, h], kt[:, h], ALU.mult).then_inc(rk_ready.sem, 1)
                dve.wait_ge(column_ready.sem, column_ready.at(it, j + 1))
                for i in range(2):
                    dve.wait_ge(scan_done.sem, scan_done.at(it, VG * j + 2 * i + 2))
                    nc.vector.tensor_tensor(ring[:, s, 2 * i:2 * i + 2], states[:, 2 * i:2 * i + 2, 0:T],
                                            rt[:, h:h + 1].broadcast_to([P, 2, T]), ALU.mult).then_inc(rs_ready.sem, 1)

            def bonus_term(it, c):
                dve.wait_ge(bonus_sum.sem, bonus_sum.at(it, c + 1))
                if c > 0:
                    dve.wait_ge(centred.sem, centred.at(it, c))
                dve.wait_ge(v_ready.sem, v_ready.at(it, c + 1))
                nc.vector.tensor_tensor(uv[:], pbonus[:], vt[:, c % 2], ALU.mult).then_inc(uv_ready.sem, 1)

            def gated(it, t, products):
                if it is None:
                    it = LAYERS * B
                else:
                    take(dve, it, ("fv", t))
                dve.wait_ge(rr_ready.sem, rr_ready.at(it, t + 1))
                nc.vector.tensor_tensor(rr[:, t], products[:], rr[:, t], ALU.mult).then_inc(gated_done.sem, 1)
                dve.wait_ge(gated_done.sem, gated_done.at(it, t + 1))
                dve.wait_ge(xres_in.sem, xres_in.at(it, 0))
                nc.vector.tensor_tensor(xres[:, t], xres[:, t], rr[:, t], ALU.add).then_inc(batch_done.sem, 1)

            def statistics(of):
                dve.wait_ge(xn_in.sem, xn_in.at(of, 16))
                for t in range(TT):
                    nc.vector.bn_stats(stats[:, 0, t], xn[:, t]).then_inc(stats_done[0].sem, 1)
                moments(of, 0)

            def shift_attention(of):
                dve.wait_ge(small_in.sem, small_in.at(of // B, 5 * 16))
                dve.wait_ge(xa_ready.sem, xa_ready.at(of, CT))
                shift_and_blend(of, 0, xa, sx, xa_ready, xxx, va, MAAX, xxx_ready)

            statistics(0)
            nc.vector.memset(xr2[:], 0.0).then_inc(xr2_ready.sem, 1)
            nc.vector.memset(kk[:], 0.0).then_inc(kk_ready.sem, 1)
            nc.vector.memset(hid2[DD + DM:], 0.0).then_inc(zeros_ready.sem, 1)
            nc.vector.memset(gate[:], 0.0).then_inc(xk2_ready.sem, 1)
            shift_attention(0)
            mix(0, 0, 3 * CT)
            for c in range(CT):
                mix_pair(0, c)
            with dve.Fori(0, LAYERS) as layer:
                for c in range(CT):
                    nc.vector.tensor_scalar(bonus[:, c], cst[:, HONES], va[:, UBONUS, c:c + 1], None,
                                            ALU.mult).then_inc(bonus_ready.sem, 1)
                with dve.Fori(0, B) as b:
                    it = layer * B + b
                    dve.wait_ge(s0_ready.sem, s0_ready.at(it, 1))
                    for c in range(CT):
                        group(it, GROUPS * c)
                        if c > 1:
                            ygate(it, c - 2)
                        if c == CT - 1:
                            gated(it, 0, bank(it, ("fv", 0)))
                            gated(it, 1, bank(it, ("fv", 1)))
                            statistics(it + 1)
                        group(it, GROUPS * c + 1)
                        if c == CT - 1:
                            bonus_term(it, c)
                            ynorm(it, c - 1)
                        if c == CT - 1:
                            gated(it, 2, bank(it, ("fv", 2)))
                            gated(it, 3, bank(it, ("fv", 3)))
                        group(it, GROUPS * c + 2)
                        if c < CT - 1:
                            bonus_term(it, c)
                        if 0 < c < CT - 1:
                            ynorm(it, c - 1)
                        if c == CT - 1:
                            ygate(it, c - 1)
                            dve.wait_ge(gate_ready.sem, gate_ready.at(it, CT))
                            shift_attention(it + 1)
                        group(it, GROUPS * c + 3)
                    dve.wait_ge(reduced.sem, reduced.at(it, NGROUP - 1))
                    mix(it + 1, 0, CT + 2)
                    ynorm(it, CT - 1)
                    mix(it + 1, CT + 2, CT + 3)
                    ygate(it, CT - 1)
                    mix(it + 1, CT + 3, 2 * CT)
                    dve.wait_ge(xres_in.sem, xres_in.at(it, 16))
                    for t in range(TT + 1):
                        if t < TT:
                            take(dve, it, ("wo", t))
                            nc.vector.tensor_tensor(xres[:, t], bank(it, ("wo", t))[:], xres[:, t], ALU.add).then_inc(xatt_ready.sem, 1)
                        if t > 0:
                            dve.wait_ge(xatt_ready.sem, xatt_ready.at(it, t))
                            nc.vector.bn_stats(stats[:, 1, t - 1], xres[:, t - 1]).then_inc(stats_done[1].sem, 1)
                    moments(it, 1)
                    mix(it + 1, 2 * CT, 2 * CT + 2)
                    mix(it + 1, 2 * CT + 2, 3 * CT)
                    mix_pair(it + 1, 0)
                    mix_pair(it + 1, 1)
                    dve.wait_ge(vectors_f_in.sem, vectors_f_in.at(it, 16))
                    shift_and_blend(it, 1, xc, sxc, xc_ready, xk2, vf, FMK, xk2_ready)
                    for c in range(2, CT):
                        mix_pair(it + 1, c)
                        for i in (2 * c - 4, 2 * c - 3):
                            blend(xr2, xc, sxc, i, vf[:, FMR, i:i + 1], xr2_ready)
            for t in range(TT):
                dve.wait_ge(last_fv.sem, t + 1)
                gated(None, t, work[t])

        @block.tensor
        def _(pe):
            pe.wait_ge(consts_in.sem, 3 * 16)

            def enter(it, job):
                if it is None:
                    return
                if TURN[job] > 0:
                    done, n = LEFT[JOBS[JOBS.index(job) - WORK]]
                    pe.wait_ge(done.sem, done.at(it, n))
                else:
                    done, n = LEFT[[j for j in JOBS if BANK[j] == BANK[job]][-1]]
                    pe.wait_ge(done.sem, done.at(it, n - done.per))

            def enter_side(of, job):
                i = SIDE.index(job)
                if i >= 2:
                    done, n = LEFT[SIDE[i - 2]]
                    pe.wait_ge(done.sem, done.at(of, n))

            def filled(ins, it, job):
                ins.then_inc(full[START[job] if it is None else BANK[job]].sem, 1)

            def filled_side(ins, job):
                ins.then_inc(side_full[SIDE_BANK[job]].sem, 1)

            def project(it, job, weight, src, column):
                enter(it, job)
                for i in range(CT):
                    ins = nc.tensor.matmul(bank(it, job)[:], weight[:, i, column:column + P], src[:, i],
                                           start=i == 0, stop=i == CT - 1)
                filled(ins, it, job)

            def project_tokens(it, job, weight, src, t, tiles=range(CT)):
                if tiles[0] == 0:
                    enter(it, job)
                for i in tiles:
                    ins = nc.tensor.matmul(bank(it, job)[:], src[:, i, P * t:P * (t + 1)], weight[:, i],
                                           start=i == 0, stop=i == CT - 1)
                if tiles[-1] == CT - 1:
                    filled(ins, it, job)

            def receptance(it, t):
                pe.wait_ge(xr2_ready.sem, xr2_ready.at(it, 0))
                pe.wait_ge(slot_in[FSLOT[FR]].sem, slot_in[FSLOT[FR]].at(it, 16))
                project_tokens(it, ("fr", t), wf[:, FSLOT[FR]], xr2, t)

            def ffn_value(it, t):
                pe.wait_ge(kk_ready.sem, kk_ready.at(it, 2))
                pe.wait_ge(slot_in[FSLOT[FV]].sem, slot_in[FSLOT[FV]].at(it, 16))
                project_tokens(it, ("fv", t), wf[:, FSLOT[FV]], kk, t)

            def ffn_key(it, c):
                ahead = c < 2
                pe.wait_ge(xk2_ready.sem, xk2_ready.at(it, CT if ahead else 0))
                pe.wait_ge(slot_in[FSLOT[FK]].sem, slot_in[FSLOT[FK]].at(it, 32 if ahead else 0))
                project(it, ("fk", c), wf[:, FSLOT[FK]], xk2, P * c)

            def output(it, tiles, n):
                pe.wait_ge(slot_in[FSLOT[WO]].sem, slot_in[FSLOT[WO]].at(it, 32))
                pe.wait_ge(yg_ready.sem, yg_ready.at(it, n))
                for t in range(TT):
                    project_tokens(it, ("wo", t), wf[:, FSLOT[WO]], yg, t, tiles)

            def turn_attention(of):
                for c in range(CT):
                    enter_side(of, ("xa", c))
                    for t in range(TT):
                        if c == 0:
                            pe.wait_ge(normed_ready[0].sem, normed_ready[0].at(of, t + 1))
                        ins = nc.tensor.transpose(side_bank(("xa", c))[:, P * t:P * (t + 1)], xn[:, t, P * c:P * (c + 1)], cst[:, IDENT])
                    filled_side(ins, ("xa", c))

            def turn_ffn(it):
                for t in range(TT):
                    pe.wait_ge(normed_ready[1].sem, normed_ready[1].at(it, t + 1))
                    for c in range(CT):
                        if t == 0:
                            enter(it, ("xc", c))
                        ins = nc.tensor.transpose(bank(it, ("xc", c))[:, P * t:P * (t + 1)], normed[:, t, P * c:P * (c + 1)], cst[:, IDENT])
                        if t == TT - 1:
                            filled(ins, it, ("xc", c))

            def hidden(of):
                job = ("maa_hidden",)
                pe.wait_ge(small_in.sem, small_in.at(of // B, 5 * 16))
                enter_side(of, job)
                for i in range(CT):
                    pe.wait_ge(xxx_ready.sem, xxx_ready.at(of, i + 1))
                    ins = nc.tensor.matmul(side_bank(job)[:], mw1[:, i, 0:P], xxx[:, i], start=i == 0, stop=i == CT - 1)
                filled_side(ins, job)

            def mixes(of, lo, hi):
                for i in range(lo, hi):
                    f, c = MIX_ORDER[i]
                    enter_side(of, MIXES[i])
                    if f == BG:
                        pe.wait_ge(hid2_ready.sem, hid2_ready.at(of, 1))
                    else:
                        pe.wait_ge(hid_ready.sem, hid_ready.at(of, 1))
                    filled_side(nc.tensor.matmul(side_bank(MIXES[i])[:], mw2[:, f, P * c:P * (c + 1)],
                                                 (hid2 if f == BG else hid)[:], start=True, stop=True), MIXES[i])

            def hidden2(of):
                job = ("hidden2",)
                pe.wait_ge(mix_ready.sem, mix_ready.at(of, CT))
                enter_side(of, job)
                for i in range(CT):
                    for j, (weight, column, src) in enumerate(((dw1, 0, mix_w), (dw1, Q, mix_w), (mw1, P, xxx))):
                        ins = nc.tensor.matmul(side_bank(job)[Q * j:Q * (j + 1), :], weight[:, i, column:column + Q], src[:, i],
                                               start=i == 0, stop=i == CT - 1)
                filled_side(ins, job)

            def project_w(it, of, c):
                pe.wait_ge(hid2_ready.sem, hid2_ready.at(of, 1))
                enter(it, ("w", c))
                filled(nc.tensor.matmul(bank(it, ("w", c))[:], dw2[:, P * c:P * (c + 1)], hid2[:], start=True, stop=True), it, ("w", c))

            def project_tile(it, of, name, c):
                which, f, n = {"v": (WV, BV, 2 * CT), "k": (WK, BK, 3 * CT), "r": (WR, BR, NF * CT), "g": (WG, BG, NF * CT)}[name]
                pe.wait_ge(weights_a_in.sem, weights_a_in.at(of // B, 4 * 16))
                pe.wait_ge(mix_ready.sem, mix_ready.at(of, n))
                project(it, (name, c), wa[:, which], MIXED[f], P * c)

            def reduce(it, j):
                c, q = j // GROUPS, j % GROUPS
                if q == 0 and c >= 2:
                    pe.wait_ge(yn_ready.sem, yn_ready.at(it, c - 1))
                pe.wait_ge(rs_ready.sem, rs_ready.at(it, 2 * (j + 1)))
                for i in range(VG):
                    ins = nc.tensor.matmul(py[c % 2][Q * i:Q * (i + 1), :], cst[:, REDUCE, Q * q:Q * (q + 1)], ring[:, j % SLOTS, i],
                                           start=q == 0, stop=q == GROUPS - 1)
                ins.then_inc(reduced.sem, 1)

            def centre(it, c):
                pe.wait_ge(raw_ready.sem, raw_ready.at(it, c + 1))
                pe.wait_ge(uv_ready.sem, uv_ready.at(it, c + 1))
                nc.tensor.matmul(py[c % 2][:], cst[:, CENTRE], uv[:], start=True, stop=False)
                nc.tensor.matmul(py[c % 2][:], cst[:, CENTRE], sq[:], start=False, stop=True).then_inc(centred.sem, 1)

            def variance(it, c):
                pe.wait_ge(sq_ready.sem, sq_ready.at(it, c + 1))
                if c > 0:
                    pe.wait_ge(yln_done.sem, yln_done.at(it, c))
                nc.tensor.matmul(pvar[:], cst[:, HMEAN], sq[:], start=True, stop=True).then_inc(var_ready.sem, 1)

            def recurrence_bonus(it, c):
                pe.wait_ge(rk_ready.sem, rk_ready.at(it, c + 1))
                if c > 0:
                    pe.wait_ge(uv_ready.sem, uv_ready.at(it, c))
                nc.tensor.matmul(pbonus[:], bonus[:, c], rk[:], start=True, stop=True).then_inc(bonus_sum.sem, 1)

            turn_attention(0)
            hidden(0)
            mixes(0, 0, CT + 3)
            hidden2(0)
            mixes(0, CT + 3, 2 * CT + 2)
            pe.wait_ge(zeros_ready.sem, 1)
            project_w(None, 0, 0)
            project_tile(None, 0, "v", 0)
            mixes(0, 2 * CT + 2, 3 * CT + 2)
            project_tile(None, 0, "k", 0)
            mixes(0, 3 * CT + 2, NF * CT)
            project_tile(None, 0, "r", 0)
            with pe.Fori(0, LAYERS) as layer:
                pe.wait_ge(bonus_ready.sem, layer * CT + CT)
                pass_gate(pe)
                with pe.Fori(0, B) as b:
                    it = layer * B + b
                    project_w(it, it, 1)
                    project_tile(it, it, "v", 1)
                    recurrence_bonus(it, 0)
                    reduce(it, 0)
                    project_tile(it, it, "k", 1)
                    reduce(it, 1)
                    project_tile(it, it, "r", 1)
                    ffn_key(it, 2)
                    reduce(it, 2)
                    ffn_key(it, 3)
                    receptance(it, 0)
                    reduce(it, 3)
                    receptance(it, 1)
                    centre(it, 0)
                    receptance(it, 2)
                    recurrence_bonus(it, 1)
                    reduce(it, 4)
                    variance(it, 0)
                    receptance(it, 3)
                    project_w(it, it, 2)
                    reduce(it, 5)
                    project_tile(it, it, "v", 2)
                    project_tile(it, it, "k", 2)
                    reduce(it, 6)
                    project_tile(it, it, "r", 2)
                    project_tile(it, it, "g", 0)
                    reduce(it, 7)
                    project_w(it, it, 3)
                    centre(it, 1)
                    project_tile(it, it, "v", 3)
                    recurrence_bonus(it, 2)
                    reduce(it, 8)
                    variance(it, 1)
                    project_tile(it, it, "k", 3)
                    reduce(it, 9)
                    project_tile(it, it, "r", 3)
                    project_tile(it, it, "g", 1)
                    reduce(it, 10)
                    project_tile(it, it, "g", 2)
                    ffn_value(it, 0)
                    reduce(it, 11)
                    ffn_value(it, 1)
                    centre(it, 2)
                    ffn_value(it, 2)
                    recurrence_bonus(it, 3)
                    reduce(it, 12)
                    variance(it, 2)
                    ffn_value(it, 3)
                    project_tile(it, it, "g", 3)
                    reduce(it, 13)
                    pe.wait_ge(yn_ready.sem, yn_ready.at(it, CT - 1))
                    pe.wait_ge(uv_ready.sem, uv_ready.at(it, CT))
                    turn_attention(it + 1)
                    output(it, range(CT - 2), CT - 2)
                    reduce(it, 14)
                    output(it, range(CT - 2, CT - 1), CT - 1)
                    hidden(it + 1)
                    mixes(it + 1, 0, 2)
                    reduce(it, 15)
                    mixes(it + 1, 2, CT)
                    centre(it, 3)
                    mixes(it + 1, CT, CT + 1)
                    variance(it, 3)
                    mixes(it + 1, CT + 1, CT + 3)
                    hidden2(it + 1)
                    mixes(it + 1, CT + 3, 2 * CT)
                    output(it, range(CT - 1, CT), CT)
                    mixes(it + 1, 2 * CT, 2 * CT + 2)
                    project_w(it, it + 1, 0)
                    mixes(it + 1, 2 * CT + 2, 3 * CT + 2)
                    turn_ffn(it)
                    mixes(it + 1, 3 * CT + 2, 3 * CT + 4)
                    project_tile(it, it + 1, "v", 0)
                    project_tile(it, it + 1, "k", 0)
                    mixes(it + 1, 3 * CT + 4, 3 * CT + 6)
                    ffn_key(it, 0)
                    mixes(it + 1, 3 * CT + 6, NF * CT)
                    ffn_key(it, 1)
                    project_tile(it, it + 1, "r", 0)
            end = LAYERS * B
            pe.wait_ge(yn_ready.sem, yn_ready.at(end, 0))
            pe.wait_ge(mterm_done.sem, mterm_done.at(end, NF * CT))
            pe.wait_ge(yln_done.sem, yln_done.at(end, 0))
            pe.wait_ge(xk2_ready.sem, xk2_ready.at(end, 0))
            pe.wait_ge(slot_in[FSLOT[FK]].sem, slot_in[FSLOT[FK]].at(end, 0))
            for c in (2, 3):
                enter(end, JOBS[c - 2])
                for i in range(CT):
                    ins = nc.tensor.matmul(work[c - 2][:], wf[:, FSLOT[FK], i, P * c:P * (c + 1)], xk2[:, i], start=i == 0, stop=i == CT - 1)
                ins.then_inc(last_fk.sem, 1)
            pe.wait_ge(xr2_ready.sem, xr2_ready.at(end, 0))
            pe.wait_ge(slot_in[FSLOT[FR]].sem, slot_in[FSLOT[FR]].at(end, 16))
            for t in range(TT):
                for i in range(CT):
                    ins = nc.tensor.matmul(last[t][:], xr2[:, i, P * t:P * (t + 1)], wf[:, FSLOT[FR], i], start=i == 0, stop=i == CT - 1)
                ins.then_inc(last_fr.sem, 1)
            pe.wait_ge(kk_ready.sem, kk_ready.at(end, 2))
            pe.wait_ge(slot_in[FSLOT[FV]].sem, slot_in[FSLOT[FV]].at(end, 16))
            for t in range(TT):
                enter(end, JOBS[t])
                for i in range(CT):
                    ins = nc.tensor.matmul(work[t][:], kk[:, i, P * t:P * (t + 1)], wf[:, FSLOT[FV], i], start=i == 0, stop=i == CT - 1)
                ins.then_inc(last_fv.sem, 1)


def program(nc):
    shapes = {
        "x": [B, T, C], "weights_a": [LAYERS, P, 4, CT, C], "weights_f": [LAYERS, P, 4, CT, C],
        "maa_w1": [LAYERS, P, CT, NF * DM], "maa_w2": [LAYERS, P, NF, C], "decay_w1": [LAYERS, P, CT, DD],
        "decay_w2": [LAYERS, P, C], "vectors_a": [LAYERS, P, NVA, CT], "vectors_f": [LAYERS, P, NVF, CT],
        "prev": [P, B, 2, CT], "s0": [P, B, CT, S], "consts": [P, NCONST, P],
    }
    args = {n: nc.dram_tensor(f"in_{n}", s, F32, kind="ExternalInput").ap() for n, s in shapes.items()}
    out = nc.dram_tensor("out", [B, T, C], F32, kind="ExternalOutput").ap()
    build(nc, *args.values(), out)


def value_order():
    row = np.arange(P)
    return S * (row % Q // GROUPS) + VG * (row % GROUPS) + row // Q


def constants():
    key_head = np.arange(P) // S
    head = value_order() // S
    same = (head[:, None] == head[None, :]).astype(np.float32)
    m = np.zeros((P, NCONST, P), np.float32)
    m[:, IDENT] = np.eye(P)
    m[:, HMEAN] = same / S
    m[:, CENTRE] = np.eye(P) - same / S
    m[:, HONES] = key_head[:, None] == head[None, :]
    column = np.arange(Q)
    for q in range(GROUPS):
        m[:, REDUCE, Q * q:Q * (q + 1)] = (key_head[:, None] == column[None, :] // GROUPS) & (column % GROUPS == q)[None, :]
    return m


def kernel(**inputs):
    import concourse.bacc as bacc
    from concourse.bass_utils import run_bass_kernel_spmd

    a = {k: np.asarray(v) for k, v in inputs.items()}

    def both(names0, names1, lay):
        return np.ascontiguousarray(np.stack([lay([a["L0_xattn_" + n] if isinstance(n, str) else n for n in names0]),
                                              lay([a["L1_xattn_" + n] if isinstance(n, str) else n for n in names1])]))

    def rows(w):
        return w.reshape(CT, P, -1).transpose(1, 0, 2)

    order = (P * np.arange(CT)[:, None] + value_order()[None, :]).reshape(-1)

    def transposed(ws):
        return np.stack([rows(w.T) for w in ws], axis=1)

    def attention(ws):
        return transposed([ws[0], ws[1], ws[2][order], ws[3][order]])

    def feed_forward(ws):
        return transposed([ws[0][:, order]] + ws[1:])

    def after(vs):
        return columns([vs[0][order], vs[1][order]] + vs[2:])

    def columns(vs):
        return np.stack([v.reshape(CT, P).T for v in vs], axis=1)

    order0, order1 = [1, 0, 3, 2, 4], [0, 1, 3, 2, 4]
    stack = a["L0_xattn_maa_stack"]


    def maa_in(names, branches):
        w = a[names].reshape(C, NF, DM)[:, branches].reshape(C, NF * DM)
        return rows(w)

    def maa_out(names, branches):
        w = a[names][branches]
        laid = np.zeros((P, NF, C), w.dtype)
        for f in range(NF):
            lo = DM * f if f < NF - 1 else DD
            laid[lo:lo + DM, f] = w[f]
        return laid

    def decay_out(ws):
        return np.concatenate([ws[0], np.zeros((P - DD, C), ws[0].dtype)])

    ctx = a["ctx_2048"]
    feeds = {
        "x": a["x"],
        "weights_a": both(["Wk", "Wr", "Wv", "Wg"], ["Wk", "Wr", "Wv", "Wg"], attention),
        "weights_f": both(["Wo", "ffn_Wk", "ffn_Wr", "ffn_Wv"], ["Wo", "fWk", "fWr", "fWv"], feed_forward),
        "maa_w1": np.stack([maa_in("L0_xattn_maa_w1", order0), maa_in("L1_xattn_maa_w1", order1)]),
        "maa_w2": np.stack([maa_out("L0_xattn_maa_w2", order0), maa_out("L1_xattn_maa_w2", order1)]),
        "decay_w1": both(["decay_w1"], ["decay_w1"], lambda w: rows(w[0])),
        "decay_w2": both(["decay_w2"], ["decay_w2"], decay_out),
        "vectors_a": both(["ln1_w", "ln1_b", "maa_x", stack[1], stack[0], stack[3], stack[2], stack[4], "time_decay", "faaaa"],
                          ["ln1_w", "ln1_b", "maa_x", "maa_w", "maa_k", "maa_r", "maa_v", "maa_g", "time_decay", "faaaa"], columns),
        "vectors_f": both(["gn_w", "gn_b", "ln2_w", "ln2_b", "ffn_maa_k", "ffn_maa_r"],
                          ["gn_w", "gn_b", "ln2_w", "ln2_b", "fmaa_k", "fmaa_r"], after),
        "prev": ctx[:, :2].reshape(B, 2, CT, P).transpose(3, 0, 1, 2),
        "s0": ctx[:, 2:2 + S].reshape(B, CT, P, S).transpose(2, 0, 1, 3),
        "consts": constants(),
    }
    feeds = {f"in_{n}": np.ascontiguousarray(v) for n, v in feeds.items()}
    nc = bacc.Bacc("TRN2", target_bir_lowering=False, num_devices=1)
    program(nc)
    result = run_bass_kernel_spmd(nc, [feeds], core_ids=[0])
    return result.results[0]["out"]
```
